# Optimizing a Trainium2 kernel written in Bass

```python
import numpy as np
import jax
import jax.numpy as jnp

def _softmax(x, axis=-1):
    return jax.nn.softmax(x, axis=axis)

def _gelu(x):
    return jax.nn.gelu(x, approximate=True)

def _silu(x):
    return jax.nn.silu(x)

def _sigmoid(x):
    return jax.nn.sigmoid(x)

def _layernorm(x, axis=-1, eps=1e-05):
    m = jnp.mean(x, axis=axis, keepdims=True)
    v = jnp.var(x, axis=axis, keepdims=True)
    return (x - m) / jnp.sqrt(v + eps)

def _scatter_add(tgt, idx, src, axis=0):
    return tgt.at[idx].add(src)

def _segment_sum(src, seg, n):
    return jax.ops.segment_sum(src, seg, n)
kernel_name = 'mk_audio_tower_d1_tok_audfeat512_r4_164f15'

def setup_inputs(seed: int=0):
    np.random.seed(seed)
    _w = jnp.asarray

    def _rec_inputs():
        import jax
        import jax.numpy as jnp
        _rk = jax.random.key(seed)
        x = 7.22013e-05 + 1.00017 * jax.random.normal(jax.random.fold_in(_rk, 1), (64, 512, 128), jnp.float32)
        return x
    x = _rec_inputs()

    def _L0_tok_setup():
        import jax, jax.numpy as jnp
        import numpy as np
        PATCH_SIZES = [8, 16, 32]
        STRIDE_RATIO = 0.5
        CTX = 512
        NUM_FEATURES = 128
        D_MODEL = 128
        BATCH = 32

        def _n_patches(p):
            s = max(1, int(p * STRIDE_RATIO))
            return (CTX - p) // s + 1

        def _extract_patches(x, patch_size, stride):
            n = (x.shape[1] - patch_size) // stride + 1
            idx = jnp.arange(n)[:, None] * stride + jnp.arange(patch_size)[None, :]
            w = x[:, idx, :]
            return w.reshape(x.shape[0], n, patch_size * x.shape[2])

        def _forward(x, W0, b0, pos0, W1, b1, pos1, W2, b2, pos2, scale_emb):
            params = [(W0, b0, pos0), (W1, b1, pos1), (W2, b2, pos2)]
            outs = []
            for i, (p, (W, b, pos)) in enumerate(zip(PATCH_SIZES, params)):
                s = max(1, int(p * STRIDE_RATIO))
                pt = _extract_patches(x, p, s)
                y = jnp.einsum('bnk,dk->bnd', pt, W) + b
                n = pt.shape[1]
                y = y + pos[:, :n, :] + scale_emb[i]
                outs.append(y)
            return jnp.concatenate(outs, axis=1)
        key = jax.random.key(seed)
        ks = jax.random.split(key, 12)
        inp = {'x': jax.random.normal(ks[0], (BATCH, CTX, NUM_FEATURES), dtype=jnp.float32)}
        for i, p in enumerate(PATCH_SIZES):
            k_in = p * NUM_FEATURES
            n = _n_patches(p)
            inp[f'W{i}'] = jax.random.normal(ks[1 + 3 * i], (D_MODEL, k_in), dtype=jnp.float32) / np.sqrt(k_in)
            inp[f'b{i}'] = jax.random.normal(ks[2 + 3 * i], (D_MODEL,), dtype=jnp.float32) / np.sqrt(k_in)
            inp[f'pos{i}'] = 0.02 * jax.random.normal(ks[3 + 3 * i], (1, n, D_MODEL), dtype=jnp.float32)
        inp['scale_emb'] = jax.random.normal(ks[10], (len(PATCH_SIZES), D_MODEL), dtype=jnp.float32)
        return inp
    _L0_tok_all = _L0_tok_setup()
    _L0_tok_in = {k: v for k, v in _L0_tok_all.items() if k in ('W0', 'b0', 'pos0', 'W1', 'b1', 'pos1', 'W2', 'b2', 'pos2', 'scale_emb')}
    del _L0_tok_all

    def _L0_attn_setup():
        import jax, jax.numpy as jnp
        import numpy as np
        HEADS = 8
        DIM_HEAD = 64
        SCALE = DIM_HEAD ** (-0.5)
        DIM = 128
        INNER = HEADS * DIM_HEAD

        def sparsemax(z):
            n = z.shape[-1]
            z_sorted = jnp.flip(jnp.sort(z, axis=-1), axis=-1)
            cssv = jnp.cumsum(z_sorted, axis=-1)
            r = jnp.arange(1, n + 1, dtype=z.dtype)
            support = 1.0 + r * z_sorted > cssv
            k = jnp.sum(support, axis=-1, keepdims=True)
            tau = (jnp.take_along_axis(cssv, k - 1, axis=-1) - 1.0) / k.astype(z.dtype)
            return jnp.maximum(z - tau, 0.0)
        key = jax.random.key(seed)
        k1, k2, k3, k4 = jax.random.split(key, 4)
        B, N = (2, 512)
        x = jax.random.normal(k1, (B, N, DIM), dtype=jnp.float32)
        W_qkv = jax.random.normal(k2, (DIM, 3 * INNER), dtype=jnp.float32) * DIM ** (-0.5)
        W_out = jax.random.normal(k3, (INNER, DIM), dtype=jnp.float32) * INNER ** (-0.5)
        b_out = jax.random.normal(k4, (DIM,), dtype=jnp.float32) * 0.02
        return {'x': x, 'W_qkv': W_qkv, 'W_out': W_out, 'b_out': b_out}
    _L0_attn_all = _L0_attn_setup()
    _L0_attn_in = {k: v for k, v in _L0_attn_all.items() if k in ('W_qkv', 'W_out', 'b_out')}
    del _L0_attn_all

    def _L0_ffn_setup():
        import jax, jax.numpy as jnp
        import numpy as np
        B, S, D, F, E, NS, K = (2, 512, 128, 512, 8, 2, 2)
        key = jax.random.key(seed)
        ks = jax.random.split(key, 6)
        scale = 0.02

        def p(k, shape):
            return jax.random.normal(k, shape, jnp.float32) * scale
        return {'x': jax.random.normal(ks[0], (B, S, D), jnp.float32), 'gate_w': p(ks[1], (E, D)), 'gate_b': jnp.zeros((E,), jnp.float32), 'sw1': p(ks[2], (NS, F, D)), 'sb1': jnp.zeros((NS, F), jnp.float32), 'sw2': p(ks[3], (NS, D, F)), 'sb2': jnp.zeros((NS, D), jnp.float32), 'rw1': p(ks[4], (E, F, D)), 'rb1': jnp.zeros((E, F), jnp.float32), 'rw2': p(ks[5], (E, D, F)), 'rb2': jnp.zeros((E, D), jnp.float32)}
    _L0_ffn_all = _L0_ffn_setup()
    _L0_ffn_in = {k: v for k, v in _L0_ffn_all.items() if k in ('gate_w', 'gate_b', 'sw1', 'sb1', 'sw2', 'sb2', 'rw1', 'rb1', 'rw2', 'rb2')}
    del _L0_ffn_all
    return {'x': x, 'L0_tok_W0': _L0_tok_in['W0'], 'L0_tok_b0': _L0_tok_in['b0'], 'L0_tok_pos0': _L0_tok_in['pos0'], 'L0_tok_W1': _L0_tok_in['W1'], 'L0_tok_b1': _L0_tok_in['b1'], 'L0_tok_pos1': _L0_tok_in['pos1'], 'L0_tok_W2': _L0_tok_in['W2'], 'L0_tok_b2': _L0_tok_in['b2'], 'L0_tok_pos2': _L0_tok_in['pos2'], 'L0_tok_scale_emb': _L0_tok_in['scale_emb'], 'L0_attn_W_qkv': _L0_attn_in['W_qkv'], 'L0_attn_W_out': _L0_attn_in['W_out'], 'L0_attn_b_out': _L0_attn_in['b_out'], 'L0_ffn_gate_w': _L0_ffn_in['gate_w'], 'L0_ffn_gate_b': _L0_ffn_in['gate_b'], 'L0_ffn_sw1': _L0_ffn_in['sw1'], 'L0_ffn_sb1': _L0_ffn_in['sb1'], 'L0_ffn_sw2': _L0_ffn_in['sw2'], 'L0_ffn_sb2': _L0_ffn_in['sb2'], 'L0_ffn_rw1': _L0_ffn_in['rw1'], 'L0_ffn_rb1': _L0_ffn_in['rb1'], 'L0_ffn_rw2': _L0_ffn_in['rw2'], 'L0_ffn_rb2': _L0_ffn_in['rb2']}

def reference(x, L0_tok_W0, L0_tok_b0, L0_tok_pos0, L0_tok_W1, L0_tok_b1, L0_tok_pos1, L0_tok_W2, L0_tok_b2, L0_tok_pos2, L0_tok_scale_emb, L0_attn_W_qkv, L0_attn_W_out, L0_attn_b_out, L0_ffn_gate_w, L0_ffn_gate_b, L0_ffn_sw1, L0_ffn_sb1, L0_ffn_sw2, L0_ffn_sb2, L0_ffn_rw1, L0_ffn_rb1, L0_ffn_rw2, L0_ffn_rb2):
    import jax
    import jax.numpy as jnp

    def _L0_tok_ref(x, W0, b0, pos0, W1, b1, pos1, W2, b2, pos2, scale_emb):
        import jax, jax.numpy as jnp
        import numpy as np
        PATCH_SIZES = [8, 16, 32]
        STRIDE_RATIO = 0.5
        CTX = 512
        NUM_FEATURES = 128
        D_MODEL = 128
        BATCH = 32

        def _n_patches(p):
            s = max(1, int(p * STRIDE_RATIO))
            return (CTX - p) // s + 1

        def _extract_patches(x, patch_size, stride):
            n = (x.shape[1] - patch_size) // stride + 1
            idx = jnp.arange(n)[:, None] * stride + jnp.arange(patch_size)[None, :]
            w = x[:, idx, :]
            return w.reshape(x.shape[0], n, patch_size * x.shape[2])

        def _forward(x, W0, b0, pos0, W1, b1, pos1, W2, b2, pos2, scale_emb):
            params = [(W0, b0, pos0), (W1, b1, pos1), (W2, b2, pos2)]
            outs = []
            for i, (p, (W, b, pos)) in enumerate(zip(PATCH_SIZES, params)):
                s = max(1, int(p * STRIDE_RATIO))
                pt = _extract_patches(x, p, s)
                y = jnp.einsum('bnk,dk->bnd', pt, W) + b
                n = pt.shape[1]
                y = y + pos[:, :n, :] + scale_emb[i]
                outs.append(y)
            return jnp.concatenate(outs, axis=1)
        return _forward(x, W0, b0, pos0, W1, b1, pos1, W2, b2, pos2, scale_emb)

    def _L0_attn_ref(x, W_qkv, W_out, b_out):
        import jax, jax.numpy as jnp
        import numpy as np
        HEADS = 8
        DIM_HEAD = 64
        SCALE = DIM_HEAD ** (-0.5)
        DIM = 128
        INNER = HEADS * DIM_HEAD

        def sparsemax(z):
            n = z.shape[-1]
            z_sorted = jnp.flip(jnp.sort(z, axis=-1), axis=-1)
            cssv = jnp.cumsum(z_sorted, axis=-1)
            r = jnp.arange(1, n + 1, dtype=z.dtype)
            support = 1.0 + r * z_sorted > cssv
            k = jnp.sum(support, axis=-1, keepdims=True)
            tau = (jnp.take_along_axis(cssv, k - 1, axis=-1) - 1.0) / k.astype(z.dtype)
            return jnp.maximum(z - tau, 0.0)
        B, N, _ = x.shape
        qkv = x @ W_qkv
        q, k, v = jnp.split(qkv, 3, axis=-1)

        def to_heads(t):
            return t.reshape(B, N, HEADS, DIM_HEAD).transpose(0, 2, 1, 3)
        q, k, v = (to_heads(q), to_heads(k), to_heads(v))
        sim = jnp.einsum('bhid,bhjd->bhij', q, k) * SCALE
        attn = sparsemax(sim)
        out = jnp.einsum('bhij,bhjd->bhid', attn, v)
        out = out.transpose(0, 2, 1, 3).reshape(B, N, INNER)
        return out @ W_out + b_out

    def _L0_ffn_ref(x, gate_w, gate_b, sw1, sb1, sw2, sb2, rw1, rb1, rw2, rb2):
        import jax, jax.numpy as jnp
        import numpy as np
        B, S, D, F, E, NS, K = (2, 512, 128, 512, 8, 2, 2)
        b, s, d = x.shape
        t = x.reshape(-1, d)
        T = t.shape[0]
        hs = jax.nn.gelu(jnp.einsum('td,nfd->ntf', t, sw1) + sb1[:, None, :], approximate=False)
        shared = jnp.einsum('ntf,ndf->td', hs, sw2) + sb2.sum(axis=0)
        logits = t @ gate_w.T + gate_b
        probs = jax.nn.softmax(logits, axis=-1)
        top_v, top_i = jax.lax.top_k(probs, K)
        cw = jnp.zeros_like(probs).at[jnp.arange(T)[:, None], top_i].add(top_v)
        hr = jax.nn.gelu(jnp.einsum('td,efd->etf', t, rw1) + rb1[:, None, :], approximate=False)
        oe = jnp.einsum('etf,edf->etd', hr, rw2) + rb2[:, None, :]
        routed = jnp.einsum('etd,te->td', oe, cw)
        return (shared + routed).reshape(b, s, d)
    h = _L0_tok_ref(x, L0_tok_W0, L0_tok_b0, L0_tok_pos0, L0_tok_W1, L0_tok_b1, L0_tok_pos1, L0_tok_W2, L0_tok_b2, L0_tok_pos2, L0_tok_scale_emb)
    h = h + _L0_attn_ref(_layernorm(h, axis=-1), L0_attn_W_qkv, L0_attn_W_out, L0_attn_b_out)
    h = h + _L0_ffn_ref(_layernorm(h, axis=-1), L0_ffn_gate_w, L0_ffn_gate_b, L0_ffn_sw1, L0_ffn_sb1, L0_ffn_sw2, L0_ffn_sb2, L0_ffn_rw1, L0_ffn_rb1, L0_ffn_rw2, L0_ffn_rb2)
    return h

_drawn_inputs = setup_inputs


def setup_inputs(seed=0):
    import zlib

    import numpy as np

    out = dict(_drawn_inputs(seed))
    spreads = {'L0_ffn_gate_b': (0.0, 0.695),
     'L0_ffn_sb1': (0.0, 0.385),
     'L0_ffn_sb2': (0.0, 0.1),
     'L0_ffn_rb1': (0.0, 0.8),
     'L0_ffn_rb2': (0.0, 0.501)}
    factors = {'L0_tok_pos0': 3.926,
     'L0_tok_b1': 3.579,
     'L0_tok_pos1': 4.493,
     'L0_tok_b2': 7.552,
     'L0_tok_pos2': 6.045,
     'L0_attn_b_out': 4.539,
     'L0_ffn_gate_w': 3.972,
     'L0_ffn_rw1': 7.121,
     'L0_ffn_rw2': 6.394}
    for name, (base, spread) in spreads.items():
        noise = np.random.default_rng([zlib.crc32(name.encode()), seed]).standard_normal(out[name].shape)
        drawn = base * np.exp(spread * noise) if base else spread * noise
        out[name] = jnp.asarray(drawn.astype(out[name].dtype))
    for name, factor in factors.items():
        out[name] = (out[name] * factor).astype(out[name].dtype)
    return out
```

```python
from contextlib import ExitStack

import concourse.bass as bass
from concourse import mybir

F32 = mybir.dt.float32
F32R = mybir.dt.float32r
I32 = mybir.dt.int32
ACT = mybir.ActivationFunctionType
ALU = mybir.AluOpType
AX = mybir.AxisListType

P = 128
PATCH = (8, 16, 32)
CTX = 512
NTOK = tuple((CTX - p) // (p // 2) + 1 for p in PATCH)
TOFF = (0, NTOK[0], NTOK[0] + NTOK[1])
T = sum(NTOK)
TP = T + 1
NB = 2
NT = NB * TP
IC = TP // 2
NI = (IC, T - IC)
BATCH = 64
G = BATCH // NB
HEADS, DH = 8, 64
HALF = HEADS // 2 * P
NEXP, NSH = 8, 2
FF = 512
FB = FF // P
BLOCKS = (NSH + NEXP) * FB
EPS = 1e-5
NEG = -3.0e38

XR, XM = 4, CTX // 4 + 4
XB = XR * XM
SB = 8
STEPS = BATCH // SB
CW = 2 * XB
WCH = 1024

LAG = 3
SLOTS = BLOCKS + LAG
UNITS = NB * HEADS
NEWTON = 24


def head_of(u):
    return u // 4, (u // 2) % 2, u % 2


def scores_at(s):
    return (s - 1) // 2 if s % 2 and 0 <= (s - 1) // 2 < UNITS else None


def transposes_at(s):
    return (s - 3) // 2 if s % 2 and 0 <= (s - 3) // 2 < UNITS else None


def values_at(s):
    return (s - 4) // 2 if s % 2 == 0 and 0 <= (s - 4) // 2 < UNITS else None


SHARED = {0: [("logits", 0, "f")], 3: [("cwT", 0, "f")],
          8: [("q", 2, "h")], 10: [("k", 2, "h")], 16: [("q", 3, "h")], 18: [("k", 3, "h")],
          11: [("mean", 0, "n")], 14: [("var", 0, "n")], 19: [("spread", 0, "n")],
          22: [("v", (0, 0, 0), "n")], 23: [("v", (0, 1, 0), "n")], 24: [("q", 0, "n")],
          26: [("v", (1, 0, 0), "n")], 27: [("v", (1, 1, 0), "n")], 28: [("k", 0, "n")],
          35: [("v", (0, 0, 1), "n")], 36: [("q", 1, "n")], 37: [("v", (0, 1, 1), "n")],
          38: [("k", 1, "n")], 41: [("v", (1, 0, 1), "n")], 42: [("v", (1, 1, 1), "n")]}
for _e in range(NEXP):
    SHARED.setdefault(5 + 4 * _e, []).append(("cwB", _e, "f"))
LN2 = {36: "mean", 38: "var", 40: "spread"}
N_SHARED = {k: sum(x[2] == k for v in SHARED.values() for x in v) for k in "fhn"}


class Body:

    def __init__(self, f, h, n, nf, nh, nn, g, i=None):
        self.f, self.h, self.n = f, h, n
        self.nf, self.nh, self.nn = nf, nh, nn
        self.g, self.i = g, i

    def at(self, count, f=0, h=0, n=0):
        static = self.nf * f + self.nh * h + self.nn * n + count
        if self.i is None:
            return static
        return self.i * (f * self.f + h * self.h + n * self.n) + static

    def shared(self):
        k = 0
        for s in sorted(SHARED):
            for what, arg, part in SHARED[s]:
                if getattr_part(self, part):
                    yield s, k, what, arg, part
                    k += 1


def getattr_part(body, part):
    return {"f": body.f, "h": body.h, "n": body.n}[part]


def wait(eng, sem, value):
    if not isinstance(value, int) or value > 0:
        eng.wait_ge(sem, value)


def attention_and_experts(nc, run, newton):
    pass


def build(nc, xT, w0T, w1T, w2T, posT, b0, b1, b2, seT, wqkT, wvT, woutT, b_out,
          gateT, gate_b, ew, eb1, sb2T, rb2, out):
    hs = nc.dram_tensor("h_scratch", (G, P, NT), F32, kind="Internal").ap()

    with ExitStack() as keep:
        def sbuf(name, shape, dt=F32, ctx=keep):
            return ctx.enter_context(nc.sbuf_tensor(name, shape, dt))

        def sem(name):
            return keep.enter_context(nc.semaphore(name))

        banks = [keep.enter_context(nc.psum_tensor(f"bank{i}", [P, 512], F32)) for i in range(8)]

        wqk_hi, wqk_lo = sbuf("wqk_hi", [P, 1024], F32R), sbuf("wqk_lo", [P, 1024], F32R)
        wvo_hi, wvo_lo = sbuf("wvo_hi", [P, 1024], F32R), sbuf("wvo_lo", [P, 1024], F32R)
        gate_hi, gate_lo = sbuf("gate_hi", [P, NEXP], F32R), sbuf("gate_lo", [P, NEXP], F32R)
        gate_raw = sbuf("gate_raw", [P, NEXP])
        rb2_raw = sbuf("rb2_raw", [NEXP, P])
        rb2_hi, rb2_lo = sbuf("rb2_hi", [NEXP, P], F32R), sbuf("rb2_lo", [NEXP, P], F32R)
        gb = sbuf("gb", [P, NEXP])
        bo = sbuf("bo", [P, 1])
        up_bias = sbuf("up_bias", [P, BLOCKS])
        sb2 = sbuf("sb2", [P, NSH])
        sb2_sum = sbuf("sb2_sum", [P, 1])
        ident = sbuf("ident", [P, P])
        id8 = sbuf("id8", [NEXP, NEXP], F32R)
        mean_w = sbuf("mean_w", [P, P])
        later = sbuf("later", [IC, NEXP * NEXP])
        e_index = sbuf("e_index", [IC, 4 * NEXP])
        rinv = sbuf("rinv", [IC, 32])
        seg = sbuf("seg", [IC, 32])
        mhalf = sbuf("mhalf", [IC, 4])
        worst = sbuf("worst", [IC, 2])
        flag = sbuf("flag", [1, 1], I32)

        with ExitStack() as first:
            def sb1(name, shape, dt=F32):
                return sbuf(name, shape, dt, first)

            wcols = (PATCH[0] * P, PATCH[1] * P, PATCH[2] * P)
            w_hi = [sb1(f"w{i}_hi", [P, n], F32R) for i, n in enumerate(wcols)]
            w_lo = [sb1(f"w{i}_lo", [P, n], F32R) for i, n in enumerate(wcols)]
            x_hi = [sb1(f"x_hi{i}", [P, SB * XB], F32R) for i in range(2)]
            x_lo = [sb1(f"x_lo{i}", [P, SB * XB], F32R) for i in range(2)]
            raw = [sb1(f"raw{i}", [P, CW]) for i in range(2)]
            stage = [sb1(f"stage{i}", [P, SB, TP]) for i in range(2)]
            table = sb1("table", [P, T])
            bvec, svec = sb1("bvec", [P, 3]), sb1("svec", [P, 3])
            wv_raw, wo_raw = sb1("wv_raw", [DH, 1024]), sb1("wo_raw", [DH, 1024])

            small = sem("small_loaded")
            memset_done = sem("memset_done")
            raw_loaded = [sem("raw_loaded0"), sem("raw_loaded1")]
            hi_done = sem("hi_done")
            lo_done = sem("lo_done")
            const_done = sem("const_done")
            fold_done = sem("fold_done")
            fold_hi = sem("fold_hi")
            fold_lo = sem("fold_lo")
            emb_done = sem("emb_done")
            emb_out = sem("emb_out")
            h_stored = [sem("h_stored0"), sem("h_stored1")]

            chunks = [("w", 0, 0)] + [("x", 0, q) for q in range(4)] + [("w", 1, 0), ("w", 1, 1)]
            chunks += [("w", 2, q) for q in range(4)] + [("qk", 0, 0)]
            FIRSTC = len(chunks)

            def chunk_no(k, q):
                return q + 1 if isinstance(k, int) and k == 0 else (k - 1) * 4 + FIRSTC + q

            def loads(sp, k, seq):
                for c, par, before, src, n in seq:
                    wait(sp, lo_done, c - 1)
                    sp.dma_start(raw[par][:, 0:n], src).then_inc(raw_loaded[par], 16)

            def x_chunks(k):
                assert FIRSTC % 2 == 0
                for q in range(4):
                    c = chunk_no(k, q)
                    yield c, q % 2, c, (k, q)

            def loaded_value(c, par):
                return (c - par) * 8 + 16

            with nc.Block() as block:
                @block.sync
                def _(sp):
                    sp.dma_start(wv_raw[:], wvT).then_inc(small, 16)
                    sp.dma_start(wo_raw[:], woutT).then_inc(small, 16)
                    for c, (kind, a, q) in enumerate(chunks):
                        wait(sp, lo_done, c - 1)
                        src = {"w": (w0T, w1T, w2T)[a][:, q * WCH:(q + 1) * WCH] if kind == "w" else None,
                               "x": xT[q], "qk": wqkT}[kind]
                        n = CW if kind == "x" else WCH
                        sp.dma_start(raw[c % 2][:, 0:n], src).then_inc(raw_loaded[c % 2], 16)

                    def step(k, par):
                        for q in range(4):
                            c = chunk_no(k + 1, q)
                            sp.wait_ge(lo_done, c - 1)
                            sp.dma_start(raw[q % 2][:, :], xT[(k + 1) * 4 + q]).then_inc(raw_loaded[q % 2], 16)
                        store(k, par)

                    def store(k, par):
                        sp.wait_ge(emb_out, k * 4 + 4)
                        sp.dma_start(hs[bass.ds(k * 4, 4)].rearrange("g p (b t) -> p g b t", b=NB),
                                     stage[par][:].rearrange("p (g b) t -> p g b t", b=NB)).then_inc(h_stored[par], 16)

                    step(0, 0)
                    with sp.Fori(0, (STEPS - 2) // 2) as i:
                        step(i * 2 + 1, 1)
                        step(i * 2 + 2, 0)
                    store(STEPS - 1, 1)
                    for par in range(2):
                        sp.wait_ge(h_stored[par], 16 * STEPS // 2)

                @block.gpsimd
                def _(pool):
                    nc.gpsimd.memset(ident[:], 0.0)
                    nc.gpsimd.memset(later[:], 0.0)
                    nc.gpsimd.memset(mean_w[:], 1.0 / P)
                    nc.gpsimd.memset(seg[:], 1.0)
                    nc.gpsimd.memset(mhalf[:], -0.5)
                    nc.gpsimd.memset(worst[:], 0.0)
                    for r in range(16):
                        nc.gpsimd.memset(rinv[:, r:r + 17:16], 1.0 / (r + 1))
                    for e in range(NEXP):
                        nc.gpsimd.memset(e_index[:, e:e + 3 * NEXP + 1:NEXP], float(e))
                    for par in range(2):
                        nc.gpsimd.memset(stage[par][:, :, T:TP], 0.0)
                    pool.drain()
                    nc.gpsimd.memset(seg[:, 0:17:16], 0.0)
                    for first_e in range(1, NEXP):
                        nc.gpsimd.memset(later[:, first_e * NEXP:first_e * NEXP + first_e], 1.0)
                    nc.gpsimd.affine_select(out=ident[:], in_=ident[:], compare_op=ALU.not_equal, fill=1.0,
                                            base=0, pattern=[[-1, P]], channel_multiplier=1)
                    pool.drain()
                    nc.gpsimd.memset(flag[:], 0).then_inc(memset_done, 1)

                @block.scalar
                def _(act):
                    for dst, src in ((gate_raw, gateT), (rb2_raw, rb2), (bo, b_out), (up_bias, eb1),
                                     (sb2, sb2T), (table, posT), (svec, seT)):
                        act.dma_start(dst[:], src).then_inc(small, 16)
                    for s, b in enumerate((b0, b1, b2)):
                        act.dma_start(bvec[:, s:s + 1], b).then_inc(small, 16)
                    act.dma_start(gb[:], gate_b.partition_broadcast(P)).then_inc(small, 16)
                    for half in range(2):
                        act.wait_ge(fold_done, half + 1)
                        nc.scalar.activation(wvo_hi[:, half * HALF:(half + 1) * HALF], banks[half][:],
                                             ACT.Copy).then_inc(fold_hi, 1)
                    for c, (kind, a, q) in enumerate(chunks):
                        act.wait_ge(raw_loaded[c % 2], loaded_value(c, c % 2))
                        dst = (x_hi[0][:, q * CW:(q + 1) * CW] if kind == "x" else wqk_hi[:] if kind == "qk"
                               else w_hi[a][:, q * WCH:(q + 1) * WCH])
                        n = CW if kind == "x" else WCH
                        nc.scalar.activation(dst, raw[c % 2][:, 0:n], ACT.Copy).then_inc(hi_done, 1)

                    def step(k, par):
                        if not isinstance(k, int) or k >= 2:
                            act.wait_ge(emb_done, k * 4 - 4)
                        for q in range(4):
                            c = chunk_no(k, q)
                            act.wait_ge(raw_loaded[q % 2], loaded_value(c, q % 2))
                            nc.scalar.activation(x_hi[par][:, q * CW:(q + 1) * CW], raw[q % 2][:],
                                                 ACT.Copy).then_inc(hi_done, 1)

                    step(1, 1)
                    with act.Fori(0, (STEPS - 2) // 2) as i:
                        step(i * 2 + 2, 0)
                        step(i * 2 + 3, 1)

                @block.vector
                def _(dve):
                    for half in range(2):
                        cols = slice(half * HALF, (half + 1) * HALF)
                        dve.wait_ge(fold_hi, half + 1)
                        nc.vector.tensor_tensor(wvo_lo[:, cols], banks[half][:], wvo_hi[:, cols].bitcast(F32),
                                                ALU.subtract).then_inc(fold_lo, 1)
                    dve.wait_ge(small, 13 * 16)
                    dve.wait_ge(memset_done, 1)
                    nc.vector.tensor_copy(gate_hi[:], gate_raw[:])
                    nc.vector.tensor_copy(rb2_hi[:], rb2_raw[:])
                    nc.vector.tensor_copy(id8[:], ident[0:NEXP, 0:NEXP])
                    nc.vector.tensor_tensor(bvec[:], bvec[:], svec[:], ALU.add)
                    nc.vector.tensor_tensor(sb2_sum[:], sb2[:, 0:1], sb2[:, 1:2], ALU.add)
                    dve.drain()
                    nc.vector.tensor_tensor(gate_lo[:], gate_raw[:], gate_hi[:].bitcast(F32), ALU.subtract)
                    nc.vector.tensor_tensor(rb2_lo[:], rb2_raw[:], rb2_hi[:].bitcast(F32), ALU.subtract)
                    for s in range(3):
                        cols = slice(TOFF[s], TOFF[s] + NTOK[s])
                        nc.vector.tensor_scalar(table[:, cols], table[:, cols], bvec[:, s:s + 1], None, ALU.add)
                    dve.drain()
                    for c, (kind, a, q) in enumerate(chunks):
                        dst, hi = ((x_lo[0][:, q * CW:(q + 1) * CW], x_hi[0][:, q * CW:(q + 1) * CW]) if kind == "x" else
                                   (wqk_lo[:], wqk_hi[:]) if kind == "qk" else
                                   (w_lo[a][:, q * WCH:(q + 1) * WCH], w_hi[a][:, q * WCH:(q + 1) * WCH]))
                        n = CW if kind == "x" else WCH
                        dve.wait_ge(hi_done, c + 1)
                        nc.vector.tensor_tensor(dst, raw[c % 2][:, 0:n], hi.bitcast(F32),
                                                ALU.subtract).then_inc(lo_done, 1)

                    def low(k, par):
                        for q in range(4):
                            dve.wait_ge(hi_done, chunk_no(k, q) + 1)
                            cols = slice(q * CW, (q + 1) * CW)
                            nc.vector.tensor_tensor(x_lo[par][:, cols], raw[q % 2][:], x_hi[par][:, cols].bitcast(F32),
                                                    ALU.subtract).then_inc(lo_done, 1)

                    def bank_out(k, par, use, dst_b, nb, s, width):
                        n, off = NTOK[s], TOFF[s]
                        dve.wait_ge(emb_done, k * 4 + use + 1)
                        src = banks[par * 4 + use][:, 0:nb * width].rearrange("p (b t) -> p b t", b=nb)[:, :, 0:n]
                        add = table[:, off:off + n].unsqueeze(1).broadcast_to([P, nb, n])
                        nc.vector.tensor_tensor(stage[par][:, dst_b:dst_b + nb, off:off + n], src, add,
                                                ALU.add).then_inc(emb_out, 1)

                    def outs(k, par, wait_store):
                        if wait_store is not None:
                            dve.wait_ge(h_stored[par], wait_store)
                        bank_out(k, par, 0, 0, 4, 0, NTOK[0] + 1)
                        bank_out(k, par, 1, 4, 4, 0, NTOK[0] + 1)
                        bank_out(k, par, 2, 0, SB, 1, NTOK[1] + 1)
                        bank_out(k, par, 3, 0, SB, 2, NTOK[2] + 1)

                    low(1, 1)
                    outs(0, 0, None)
                    low(2, 0)
                    outs(1, 1, None)
                    with dve.Fori(0, (STEPS - 4) // 2) as i:
                        low(i * 2 + 3, 1)
                        outs(i * 2 + 2, 0, i * 16 + 16)
                        low(i * 2 + 4, 0)
                        outs(i * 2 + 3, 1, i * 16 + 16)
                    low(STEPS - 1, 1)
                    outs(STEPS - 2, 0, (STEPS // 2 - 1) * 16)
                    outs(STEPS - 1, 1, (STEPS // 2 - 1) * 16)

                @block.tensor
                def _(pe):
                    pe.wait_ge(small, 13 * 16)
                    for half in range(2):
                        for j in range(HEADS // 2):
                            h = half * HEADS // 2 + j
                            last = nc.tensor.matmul(banks[half][:, j * P:(j + 1) * P], wv_raw[:, h * P:(h + 1) * P],
                                                    wo_raw[:, h * P:(h + 1) * P], start=True, stop=True)
                        last.then_inc(fold_done, 1)

                    def products(out_ap, s, j, par, b0_, nb, n, first_, last_):
                        st = PATCH[s] // 8
                        def moving(x):
                            v = x[par][:].rearrange("p (b r m) -> p b r m", b=SB, r=XR)
                            return v[:, b0_:b0_ + nb, j % XR, j // XR:j // XR + st * (n - 1) + 1:st]
                        cols = slice(j * P, (j + 1) * P)
                        nc.tensor.matmul(out_ap, w_hi[s][:, cols], moving(x_hi), start=first_, stop=False)
                        nc.tensor.matmul(out_ap, w_hi[s][:, cols], moving(x_lo), start=False, stop=False)
                        return nc.tensor.matmul(out_ap, w_lo[s][:, cols], moving(x_hi), start=False, stop=last_)

                    def step(k, par, cold=False):
                        if not isinstance(k, int) or k >= 2:
                            pe.wait_ge(emb_out, k * 4 - 4)
                        if cold:
                            pe.wait_ge(fold_lo, 2)
                        for use, s, b0_, nb in ((0, 0, 0, 4), (1, 0, 4, 4), (2, 1, 0, SB), (3, 2, 0, SB)):
                            n = NTOK[s] + 1
                            if use < 2:
                                pe.wait_ge(lo_done, chunk_no(k, 2 * use + 1) + 1)
                            elif cold:
                                pe.wait_ge(lo_done, 7 if s == 1 else 11)
                            o = banks[par * 4 + use][:, 0:nb * n]
                            for j in range(PATCH[s]):
                                last = products(o, s, j, par, b0_, nb, n, j == 0, j == PATCH[s] - 1)
                            last.then_inc(emb_done, 1)

                    step(0, 0, True)
                    step(1, 1)
                    with pe.Fori(0, (STEPS - 2) // 2) as i:
                        step(i * 2 + 2, 0)
                        step(i * 2 + 3, 1)

        with ExitStack() as second:
            def sb2_(name, shape, dt=F32):
                return sbuf(name, shape, dt, second)

            NE = (NSH + NEXP)
            ew_hi, ew_lo = sb2_("ew_hi", [P, NE * WCH], F32R), sb2_("ew_lo", [P, NE * WCH], F32R)
            rings = sb2_("rings", [P, 7 * NT])
            cwB = [rings[:, i * NT:(i + 1) * NT] for i in range(3)]
            g_raw = [rings[:, (3 + i) * NT:(4 + i) * NT] for i in range(2)]
            tmp = [rings[:, (5 + i) * NT:(6 + i) * NT] for i in range(2)]
            wst = [rings[:, i * WCH:(i + 1) * WCH] for i in range(3)]
            x1_hi, x1_lo = sb2_("x1_hi", [P, NT], F32R), sb2_("x1_lo", [P, NT], F32R)
            x2_hi, x2_lo = sb2_("x2_hi", [P, NT], F32R), sb2_("x2_lo", [P, NT], F32R)
            qk_hi = {(w, r): sb2_(f"{w}_hi{r}", [P, NT], F32R) for w in "qk" for r in range(2)}
            qk_lo = {(w, r): sb2_(f"{w}_lo{r}", [P, NT], F32R) for w in "qk" for r in range(2)}
            v_hi = sb2_("v_hi", [IC, NB, 2, 2 * HALF], F32R)
            v_lo = sb2_("v_lo", [IC, NB, 2, 2 * HALF], F32R)
            a = [sb2_(f"a{r}", [IC, 2, TP]) for r in range(2)]
            at_hi = [sb2_(f"at_hi{r}", [IC, 2, TP], F32R) for r in range(2)]
            at_lo = [sb2_(f"at_lo{r}", [IC, 2, TP], F32R) for r in range(2)]
            g_hi = [sb2_(f"g_hi{r}", [P, NT], F32R) for r in range(3)]
            g_lo = [sb2_(f"g_lo{r}", [P, NT], F32R) for r in range(3)]
            h_next, h_res, h2, acc = (sb2_(n, [P, NT]) for n in ("h_next", "h_res", "h2", "acc"))
            xc, sq = sb2_("xc", [P, NT]), sb2_("sq", [P, NT])
            cwT_hi, cwT_lo = sb2_("cwT_hi", [NEXP, NT], F32R), sb2_("cwT_lo", [NEXP, NT], F32R)
            z_rest = [sb2_(f"z_rest{i}", [IC, T]) for i in range(2)]
            cand = [sb2_(f"cand{r}", [IC, 2, 16]) for r in range(2)]
            sums, taus = sb2_("sums", [IC, 32]), sb2_("taus", [IC, 32])
            ntau = [sb2_(f"ntau{r}", [IC, 2]) for r in range(2)]
            over = sb2_("over", [IC, 2])
            ve, rs = sb2_("ve", [IC, 4]), sb2_("rs", [IC, 4])
            lg, ex, pr, cw = (sb2_(n, [IC, 4, NEXP]) for n in ("lg", "ex", "pr", "cw"))
            lmax, lsum, lrec = (sb2_(n, [IC, 4]) for n in ("lmax", "lsum", "lrec"))
            bigger = sb2_("bigger", [IC, 4, NEXP * NEXP])
            pairs = sb2_("pairs", [IC, 4, NEXP * NEXP])
            s_col, s_row, rank = (sb2_(n, [IC, 4, NEXP]) for n in ("s_col", "s_row", "rank"))
            zero_row = sb2_("zero_row", [IC, T])
            nsum, ncnt, nrec = (sb2_(n, [IC, 2]) for n in ("nsum", "ncnt", "nrec"))

            z = banks[0:2]
            at = banks[2]
            y = banks[3]
            sh = banks[4]
            up = banks[5:7]
            dn = banks[7]

            ready = sem("ready")
            w_loaded = [sem(f"w_loaded{i}") for i in range(3)]
            w_hi_done = sem("w_hi_done")
            w_lo_done = sem("w_lo_done")
            next_loaded = sem("next_loaded")
            res_loaded = sem("res_loaded")
            out_stored = sem("out_stored")
            sh_done = sem("sh_done")
            sh_hi = sem("sh_hi")
            sh_free = sem("sh_free")
            ln1_xc, ln2_xc = sem("ln1_xc"), sem("ln2_xc")
            ln1_sq, ln2_sq = sem("ln1_sq"), sem("ln2_sq")
            ln1_ve, ln2_ve = sem("ln1_ve"), sem("ln2_ve")
            ln1_rs, ln2_rs = sem("ln1_rs"), sem("ln2_rs")
            x1_done, x2_done = sem("x1_done"), sem("x2_done")
            ln2_pe = sem("ln2_pe")
            z_done = sem("z_done")
            z_read = sem("z_read")
            ntau_done = sem("ntau_done")
            over_done = sem("over_done")
            relu_done = sem("relu_done")
            at_done = sem("at_done")
            at_hi_done = sem("at_hi_done")
            at_lo_done = sem("at_lo_done")
            y_done = sem("y_done")
            h2_done = sem("h2_done")
            up_done = sem("up_done")
            gelu_done = sem("gelu_done")
            g_hi_done = sem("g_hi_done")
            g_lo_done = sem("g_lo_done")
            dn_done = sem("dn_done")
            comb_done = sem("comb_done")
            acc_done = sem("acc_done")
            lg_done = sem("lg_done")
            ex_done = sem("ex_done")
            bigger_done = sem("bigger_done")
            pairs_done = sem("pairs_done")
            cw_done = sem("cw_done")
            flag_sum = sem("flag_sum")
            flag_done = sem("flag_done")
            worst_done = sem("worst_done")

            HAS_HI = ("q", "k", "v", "cwT")

            def hi_uses(body):
                n = {p: sum(x[2] == p and x[0] in HAS_HI for v in SHARED.values() for x in v) for p in "fhn"}
                return n

            N_HI = hi_uses(None)

            def sh_at(body, n):
                return body.at(n, f=N_SHARED["f"], h=N_SHARED["h"], n=N_SHARED["n"])

            def sh_hi_at(body, n):
                return body.at(n, f=N_HI["f"], h=N_HI["h"], n=N_HI["n"])

            def uses(body, s):
                k = khi = 0
                found = []
                for t in sorted(SHARED):
                    for what, arg, part in SHARED[t]:
                        if {"f": body.f, "h": body.h, "n": body.n}[part]:
                            if t == s:
                                found.append((k, khi, what, arg))
                            k += 1
                            khi += what in HAS_HI
                return found

            def bodies(eng, emit, base, newton):
                nb = base * G
                emit(Body(0, 0, 1, nb, nb, nb, -1), newton)
                emit(Body(0, 1, 1, nb, nb, nb + 1, 0), newton)
                emit(Body(1, 1, 1, nb, nb + 1, nb + 2, 1), newton)
                with eng.Fori(0, G - 3) as i:
                    emit(Body(1, 1, 1, nb + 1, nb + 2, nb + 3, i + 2, i), newton)
                emit(Body(1, 1, 0, nb + G - 2, nb + G - 1, nb + G, G - 1), newton)
                emit(Body(1, 0, 0, nb + G - 1, nb + G, nb + G, G), newton)

            def either(eng, flag_reg, general):
                with eng.If(flag_reg > 0):
                    general()
                with eng.Else():
                    eng.nop()

            def sp_body(sp, body, newton):
                if body.n:
                    wait(sp, ln1_xc, body.at(0, n=1))
                    sp.dma_start(h_next[:], hs[body.g + 1]).then_inc(next_loaded, 16)
                if body.h:
                    wait(sp, h2_done, body.at(0, h=1))
                    sp.dma_start(h_res[:], hs[body.g]).then_inc(res_loaded, 16)
                if body.f:
                    sp.wait_ge(acc_done, body.at(8, f=8))
                    sp.dma_start(out[body.g - 1], acc[:]).then_inc(out_stored, 16)

            def three(out_ap, s_hi, s_lo, m_hi, m_lo, start=True, stop=True, share=False):
                kw = {"skip_group_check": True} if share else {}
                nc.tensor.matmul(out_ap, s_hi, m_hi, start=start, stop=False, **kw)
                nc.tensor.matmul(out_ap, s_hi, m_lo, start=False, stop=False, **kw)
                return nc.tensor.matmul(out_ap, s_lo, m_hi, start=False, stop=stop, **kw)

            def ln_product(pe, bank, what, src):
                if what == "mean":
                    return nc.tensor.matmul(bank[:, 0:NT], mean_w[:], src[:], start=True, stop=True)
                for c in range(4):
                    cols = slice(c * IC, (c + 1) * IC)
                    if what == "var":
                        last = nc.tensor.matmul(bank[0:IC, c:c + 1], sq[:, cols], mean_w[:, 0:1],
                                                start=True, stop=True)
                    else:
                        last = nc.tensor.matmul(bank[:, cols], rs[:, c:c + 1].broadcast_to([IC, P]),
                                                ident[0:IC, 0:IC], start=True, stop=True)
                return last

            def pe_shared(pe, body, k, what, arg):
                wait(pe, sh_free, sh_at(body, k))
                if what == "logits":
                    pe.wait_ge(x2_done, body.at(1, f=1))
                    for c in range(4):
                        cols = slice(c * IC, (c + 1) * IC)
                        last = three(sh[0:IC, c * NEXP:(c + 1) * NEXP], x2_hi[:, cols], x2_lo[:, cols],
                                     gate_hi[:], gate_lo[:])
                elif what == "cwT":
                    pe.wait_ge(cw_done, body.at(1, f=1))
                    for c in range(4):
                        last = nc.tensor.transpose(sh[0:NEXP, c * IC:(c + 1) * IC], cw[:, c, :], ident[0:IC, 0:IC])
                elif what == "cwB":
                    sel = id8[:, arg:arg + 1].broadcast_to([NEXP, P])
                    nc.tensor.matmul(sh[:, 0:NT], sel, cwT_hi[:], start=True, stop=False)
                    last = nc.tensor.matmul(sh[:, 0:NT], sel, cwT_lo[:], start=False, stop=True)
                elif what in "qk":
                    cols = slice((what == "k") * 512 + arg * P, (what == "k") * 512 + (arg + 1) * P)
                    last = three(sh[:, 0:NT], wqk_hi[:, cols], wqk_lo[:, cols], x1_hi[:], x1_lo[:])
                elif what == "v":
                    b, c, half = arg
                    rows = slice(b * TP + c * IC, b * TP + (c + 1) * IC)
                    cols = slice(half * HALF, (half + 1) * HALF)
                    last = three(sh[0:IC, :], x1_hi[:, rows], x1_lo[:, rows], wvo_hi[:, cols], wvo_lo[:, cols])
                else:
                    if what == "mean":
                        pe.wait_ge(next_loaded, body.at(1, n=1) * 16)
                    elif what == "var":
                        pe.wait_ge(ln1_sq, body.at(1, n=1))
                    else:
                        pe.wait_ge(ln1_rs, body.at(1, n=1))
                    last = ln_product(pe, sh, what, h_next)
                last.then_inc(sh_done, 1)

            def pe_body(pe, body, newton):
                for s in range(SLOTS):
                    if body.f and 0 <= s - LAG < BLOCKS:
                        d = s - LAG
                        e, fb = divmod(d, FB)
                        cols = slice(e * WCH + 512 + fb * P, e * WCH + 512 + (fb + 1) * P)
                        if (d % FB == 0 and e != 1):
                            wait(pe, comb_done, body.at(max(e - 1, 0), f=9))
                        pe.wait_ge(g_lo_done, body.at(d + 1, f=BLOCKS))
                        last = three(dn[:, 0:NT], ew_hi[:, cols], ew_lo[:, cols], g_hi[d % 3][:], g_lo[d % 3][:],
                                     start=fb == 0 and e != 1, stop=fb == FB - 1 and e > 1)
                        if e == 1 and fb == FB - 1:
                            pe.wait_ge(sh_free, sh_at(body, 2))
                            last = three(dn[:, 0:NT], rb2_hi[:], rb2_lo[:], cwT_hi[:], cwT_lo[:], start=False)
                        if fb == FB - 1 and e >= 1:
                            last.then_inc(dn_done, 1)
                    if body.f and s < BLOCKS:
                        e, fb = divmod(s, FB)
                        cols = slice(e * WCH + fb * P, e * WCH + (fb + 1) * P)
                        if s == 0:
                            pe.wait_ge(x2_done, body.at(1, f=1))
                        wait(pe, gelu_done, body.at(s - 1, f=BLOCKS))
                        three(up[s % 2][:, 0:NT], ew_hi[:, cols], ew_lo[:, cols], x2_hi[:], x2_lo[:]).then_inc(up_done, 1)
                    u = scores_at(s)
                    if body.h and u is not None:
                        p, b, j = head_of(u)
                        r, rows = p % 2, slice(j * DH, (j + 1) * DH)
                        wait(pe, relu_done, body.at(u - 1, h=UNITS))
                        if u == 0:
                            wait(pe, x2_done, body.at(0, h=1))
                        pe.wait_ge(sh_free, sh_at(body, 0 if p < 2 else next(
                            k for t in SHARED for k, _, w, g_ in uses(body, t) if (w, g_) == ("k", p)) + 1))
                        for c in range(2):
                            q0 = b * TP + c * IC
                            last = three(z[u % 2][0:NI[c], c * TP:(c + 1) * TP],
                                         qk_hi["q", r][rows, q0:q0 + NI[c]], qk_lo["q", r][rows, q0:q0 + NI[c]],
                                         qk_hi["k", r][rows, b * TP:(b + 1) * TP], qk_lo["k", r][rows, b * TP:(b + 1) * TP])
                        last.then_inc(z_done, 1)
                    u = transposes_at(s)
                    if body.h and u is not None:
                        wait(pe, at_lo_done, body.at(u, h=UNITS))
                        pe.wait_ge(relu_done, body.at(u + 1, h=UNITS))
                        for jc in range(2):
                            for c in range(2):
                                last = nc.tensor.transpose(
                                    at[0:NI[jc], jc * TP + c * IC:jc * TP + c * IC + NI[c]],
                                    a[u % 2][0:NI[c], c, jc * IC:jc * IC + NI[jc]], ident[0:NI[c], 0:NI[c]])
                        last.then_inc(at_done, 1)
                    u = values_at(s)
                    if body.h and u is not None:
                        p, b, j = head_of(u)
                        cols = slice((2 * p + j) * P, (2 * p + j + 1) * P)
                        pe.wait_ge(at_lo_done, body.at(u + 1, h=UNITS))
                        if u == 0:
                            wait(pe, h2_done, body.at(0, h=1))
                        for jc in range(2):
                            n = NI[jc]
                            last = three(y[:, b * TP:(b + 1) * TP], v_hi[0:n, b, jc, cols], v_lo[0:n, b, jc, cols],
                                         at_hi[u % 2][0:n, jc, :], at_lo[u % 2][0:n, jc, :],
                                         start=u == 0 and jc == 0, stop=p == 3 and j == 1 and jc == 1, share=True)
                        if u == UNITS - 1:
                            last.then_inc(y_done, 1)
                    if body.h and s in LN2:
                        what = LN2[s]
                        if what == "mean":
                            pe.wait_ge(h2_done, body.at(1, h=1))
                        elif what == "var":
                            pe.wait_ge(ln2_sq, body.at(1, h=1))
                        else:
                            pe.wait_ge(ln2_rs, body.at(1, h=1))
                        ln_product(pe, z[0], what, h2).then_inc(ln2_pe, 1)
                    for k, _, what, arg in uses(body, s):
                        pe_shared(pe, body, k, what, arg)

            def act_shared(act, body, k, khi, what, arg):
                if what in HAS_HI:
                    act.wait_ge(sh_done, sh_at(body, k + 1))
                    if what == "v":
                        b, c, half = arg
                        dst, src = v_hi[:, b, c, half * HALF:(half + 1) * HALF], sh[0:IC, :]
                    elif what == "cwT":
                        dst, src = cwT_hi[:], sh[0:NEXP, 0:NT]
                    else:
                        dst, src = qk_hi[what, arg % 2][:], sh[:, 0:NT]
                    nc.scalar.activation(dst, src, ACT.Copy,
                                         scale=DH ** -0.5 if what == "q" else 1.0).then_inc(sh_hi, 1)
                elif what == "cwB":
                    wait(act, comb_done, body.at(arg - 1, f=9))
                    act.wait_ge(sh_done, sh_at(body, k + 1))
                    nc.scalar.activation(cwB[arg % 3], sh[:, 0:NT], ACT.Copy).then_inc(sh_free, 1)
                elif what == "var":
                    pass
                elif what == "mean":
                    act.wait_ge(ln1_xc, body.at(1, n=1))
                    nc.scalar.activation(sq[:], xc[:], ACT.Square).then_inc(ln1_sq, 1)

            def act_body(act, body, newton):
                for s in range(SLOTS):
                    if body.f and s < BLOCKS:
                        wait(act, g_lo_done, body.at(s - 1, f=BLOCKS))
                        act.wait_ge(up_done, body.at(s + 1, f=BLOCKS))
                        nc.scalar.activation(g_raw[s % 2], up[s % 2][:, 0:NT], ACT.Gelu,
                                             bias=up_bias[:, s:s + 1]).then_inc(gelu_done, 1)
                    if body.f and s == 1:
                        act.wait_ge(lg_done, body.at(1, f=1))
                        nc.scalar.activation(ex[:], lg[:], ACT.Exp).then_inc(ex_done, 1)
                    u = scores_at(s - 1)
                    if body.h and u is not None:
                        act.wait_ge(ntau_done, body.at(u + 1, h=UNITS))
                        for c in range(2):
                            last = nc.scalar.activation(a[u % 2][0:NI[c], c, 0:T], z[u % 2][0:NI[c], c * TP:c * TP + T],
                                                        ACT.Relu, bias=ntau[u % 2][0:NI[c], c:c + 1])
                        last.then_inc(relu_done, 1)
                    u = transposes_at(s)
                    if body.h and u is not None:
                        act.wait_ge(at_done, body.at(u + 1, h=UNITS))
                        nc.scalar.activation(at_hi[u % 2][:, :, 0:T], at[0:IC, 0:NT].rearrange("p (c t) -> p c t", c=2)[:, :, 0:T],
                                             ACT.Copy).then_inc(at_hi_done, 1)
                    if body.h and LN2.get(s) == "mean":
                        act.wait_ge(ln2_xc, body.at(1, h=1))
                        nc.scalar.activation(sq[:], xc[:], ACT.Square).then_inc(ln2_sq, 1)
                    for k, khi, what, arg in uses(body, s):
                        act_shared(act, body, k, khi, what, arg)

            def act_weights(act):
                for e in range(NE):
                    act.wait_ge(w_loaded[e % 3], 16 * (e // 3 + 1))
                    nc.scalar.activation(ew_hi[:, e * WCH:(e + 1) * WCH], wst[e % 3], ACT.Copy).then_inc(w_hi_done, 1)

            def ln_dve(dve, bank, what, src, xc_sem, ve_sem, x_hi_, x_lo_, done, n, x_sem, pe_sem_wait, free):
                pe_sem_wait()
                if what == "mean":
                    i = nc.vector.tensor_tensor(xc[:], src[:], bank[:, 0:NT], ALU.subtract)
                    i.then_inc(xc_sem, 1)
                elif what == "var":
                    i = nc.vector.tensor_scalar(ve[:], bank[0:IC, 0:4], EPS, None, ALU.add)
                    i.then_inc(ve_sem, 1)
                else:
                    nc.vector.tensor_tensor(xc[:], xc[:], bank[:, 0:NT], ALU.mult)
                    dve.drain()
                    nc.vector.tensor_copy(x_hi_[:], xc[:])
                    dve.drain()
                    i = nc.vector.tensor_tensor(x_lo_[:], xc[:], x_hi_[:].bitcast(F32), ALU.subtract)
                    i.then_inc(x_sem, 1)
                return i

            def dve_shared(dve, body, k, khi, what, arg):
                done = sh_at(body, k + 1)
                if what in HAS_HI:
                    dve.wait_ge(sh_hi, sh_hi_at(body, khi + 1))
                    if what == "v":
                        b, c, half = arg
                        cols = slice(half * HALF, (half + 1) * HALF)
                        nc.vector.tensor_tensor(v_lo[:, b, c, cols], sh[0:IC, :], v_hi[:, b, c, cols].bitcast(F32),
                                                ALU.subtract).then_inc(sh_free, 1)
                    elif what == "q":
                        nc.vector.scalar_tensor_tensor(
                            out=qk_lo["q", arg % 2][:], in0=sh[:, 0:NT], scalar=DH ** -0.5,
                            in1=qk_hi["q", arg % 2][:].bitcast(F32), op0=ALU.mult, op1=ALU.subtract).then_inc(sh_free, 1)
                    elif what == "k":
                        nc.vector.tensor_tensor(qk_lo["k", arg % 2][:], sh[:, 0:NT], qk_hi["k", arg % 2][:].bitcast(F32),
                                                ALU.subtract).then_inc(sh_free, 1)
                    else:
                        nc.vector.tensor_tensor(cwT_lo[:], sh[0:NEXP, 0:NT], cwT_hi[:].bitcast(F32),
                                                ALU.subtract).then_inc(sh_free, 1)
                elif what == "logits":
                    dve.wait_ge(sh_done, done)
                    nc.vector.tensor_tensor(lg[:], sh[0:IC, 0:4 * NEXP].rearrange("p (c e) -> p c e", c=4),
                                            gb[0:IC, :].unsqueeze(1).broadcast_to([IC, 4, NEXP]),
                                            ALU.add).then_inc(sh_free, 1)
                    dve.drain()
                    nc.vector.tensor_reduce(lmax[:], lg[:], AX.X, ALU.max)
                    dve.drain()
                    nc.vector.tensor_tensor(lg[:], lg[:], lmax[:].unsqueeze(2).broadcast_to([IC, 4, NEXP]),
                                            ALU.subtract).then_inc(lg_done, 1)
                elif what == "mean":
                    dve.wait_ge(sh_done, done)
                    nc.vector.tensor_tensor(xc[:], h_next[:], sh[:, 0:NT], ALU.subtract).then_inc(ln1_xc, 1)
                    nc.vector.drain().then_inc(sh_free, 1)
                elif what == "var":
                    dve.wait_ge(sh_done, done)
                    nc.vector.tensor_scalar(ve[:], sh[0:IC, 0:4], EPS, None, ALU.add).then_inc(ln1_ve, 1)
                    nc.vector.drain().then_inc(sh_free, 1)
                elif what == "spread":
                    dve.wait_ge(sh_done, done)
                    nc.vector.tensor_tensor(xc[:], xc[:], sh[:, 0:NT], ALU.mult)
                    dve.drain()
                    nc.vector.tensor_copy(x1_hi[:], xc[:])
                    dve.drain()
                    nc.vector.tensor_tensor(x1_lo[:], xc[:], x1_hi[:].bitcast(F32), ALU.subtract).then_inc(sh_free, 1)

            def softmax(dve, body):
                dve.wait_ge(ex_done, body.at(1, f=1))
                nc.vector.tensor_reduce(lsum[:], ex[:], AX.X, ALU.add)
                dve.drain()
                nc.vector.reciprocal(lrec[:], lsum[:])
                dve.drain()
                nc.vector.tensor_tensor(pr[:], ex[:], lrec[:].unsqueeze(2).broadcast_to([IC, 4, NEXP]),
                                        ALU.mult)
                dve.drain()
                nc.vector.tensor_tensor(bigger[:].rearrange("p c (i e) -> p c i e", i=NEXP),
                                        pr[:].unsqueeze(3).broadcast_to([IC, 4, NEXP, NEXP]),
                                        pr[:].unsqueeze(2).broadcast_to([IC, 4, NEXP, NEXP]),
                                        ALU.is_gt).then_inc(bigger_done, 1)

            def top2(dve, body):
                dve.wait_ge(pairs_done, body.at(1, f=1))
                nc.vector.tensor_reduce(s_col[:], pairs[:].rearrange("p c (i e) -> p c e i", i=NEXP), AX.X, ALU.add)
                nc.vector.tensor_reduce(s_row[:], pairs[:].rearrange("p c (i e) -> p c i e", i=NEXP), AX.X, ALU.add)
                dve.drain()
                nc.vector.tensor_tensor(rank[:], s_col[:], s_row[:], ALU.subtract)
                dve.drain()
                nc.vector.tensor_tensor(rank[:], rank[:], e_index[:].rearrange("p (c e) -> p c e", c=4), ALU.add)
                dve.drain()
                nc.vector.scalar_tensor_tensor(out=cw[:], in0=rank[:], scalar=1.5, in1=pr[:],
                                               op0=ALU.is_lt, op1=ALU.mult).then_inc(cw_done, 1)

            def threshold(dve, body, u, newton):
                zu, cd = z[u % 2], cand[u % 2]
                def own(n):
                    dve.wait_ge(z_read, body.at(3 * u + n, h=3 * UNITS))
                wait(dve, over_done, body.at(u - 1, h=UNITS))
                dve.wait_ge(z_done, body.at(u + 1, h=UNITS))
                dve.nop(nofuse=True)
                for c in range(2):
                    nc.vector.max(cd[0:NI[c], c, 0:8], zu[0:NI[c], c * TP:c * TP + T])
                dve.drain()
                for c in range(2):
                    nc.vector.match_replace(z_rest[c][0:NI[c], :], cd[0:NI[c], c, 0:8],
                                            zu[0:NI[c], c * TP:c * TP + T], NEG)
                dve.drain()
                for c in range(2):
                    last = nc.vector.max(cd[0:NI[c], c, 8:16], z_rest[c][0:NI[c], :])
                last.then_inc(z_read, 1)
                own(1)
                nc.vector.tensor_tensor_scan(sums[:], seg[:], cd[:].rearrange("p c r -> p (c r)"), 0.0,
                                             ALU.mult, ALU.add).then_inc(z_read, 1)
                own(2)
                nc.vector.scalar_tensor_tensor(out=taus[:], in0=sums[:], scalar=-1.0, in1=rinv[:],
                                               op0=ALU.add, op1=ALU.mult).then_inc(z_read, 1)
                own(3)
                i = nc.vector.tensor_reduce(ntau[u % 2][:], taus[:].rearrange("p (c r) -> p c r", c=2), AX.X, ALU.max,
                                            negate=True)
                if newton:
                    dve.drain()
                    with dve.Fori(0, NEWTON) as _:
                        for c in range(2):
                            n = NI[c]
                            zc, nt = zu[0:n, c * TP:c * TP + T], ntau[u % 2][0:n, c:c + 1]
                            nc.vector.tensor_scalar(z_rest[c][0:n, :], zc, nt, 0.0, ALU.add, ALU.max)
                            dve.drain()
                            nc.vector.tensor_reduce(nsum[0:n, c:c + 1], z_rest[c][0:n, :], AX.X, ALU.add)
                            dve.drain()
                            nc.vector.tensor_scalar(z_rest[c][0:n, :], z_rest[c][0:n, :], 0.0, None, ALU.is_gt)
                            dve.drain()
                            nc.vector.tensor_reduce(ncnt[0:n, c:c + 1], z_rest[c][0:n, :], AX.X, ALU.add)
                            dve.drain()
                            nc.vector.reciprocal(nrec[0:n, c:c + 1], ncnt[0:n, c:c + 1])
                            dve.drain()
                            nc.vector.scalar_tensor_tensor(out=nsum[0:n, c:c + 1], in0=nsum[0:n, c:c + 1], scalar=-1.0,
                                                           in1=nrec[0:n, c:c + 1], op0=ALU.add, op1=ALU.mult)
                            dve.drain()
                            nc.vector.tensor_tensor(nt, nt, nsum[0:n, c:c + 1], ALU.subtract)
                            dve.drain()
                    i = nc.vector.tensor_copy(nrec[0:1, 0:1], nrec[0:1, 0:1])
                i.then_inc(ntau_done, 1)

            def dve_body(dve, body, newton):
                for s in range(SLOTS + 1):
                    if body.f and s < BLOCKS:
                        dve.wait_ge(gelu_done, body.at(s + 1, f=BLOCKS))
                        nc.vector.tensor_copy(g_hi[s % 3][:], g_raw[s % 2]).then_inc(g_hi_done, 1)
                    u = scores_at(s)
                    if body.h and u is not None:
                        threshold(dve, body, u, newton)
                    u = transposes_at(s)
                    if body.h and u is not None:
                        dve.wait_ge(at_hi_done, body.at(u + 1, h=UNITS))
                        nc.vector.tensor_tensor(at_lo[u % 2][:, :, 0:T], at[0:IC, 0:NT].rearrange("p (c t) -> p c t", c=2)[:, :, 0:T],
                                                at_hi[u % 2][:, :, 0:T].bitcast(F32), ALU.subtract).then_inc(at_lo_done, 1)
                    if body.h and s == 35:
                        dve.wait_ge(res_loaded, body.at(1, h=1) * 16)
                        dve.wait_ge(y_done, body.at(1, h=1))
                        nc.vector.scalar_tensor_tensor(out=h2[:], in0=y[:, 0:NT], scalar=bo[:], in1=h_res[:],
                                                       op0=ALU.add, op1=ALU.add).then_inc(h2_done, 1)
                    if body.h and s in LN2:
                        done = body.at({"mean": 1, "var": 2, "spread": 3}[LN2[s]], h=3)
                        dve.wait_ge(ln2_pe, done)
                        if LN2[s] == "mean":
                            nc.vector.tensor_tensor(xc[:], h2[:], z[0][:, 0:NT], ALU.subtract).then_inc(ln2_xc, 1)
                        elif LN2[s] == "var":
                            nc.vector.tensor_scalar(ve[:], z[0][0:IC, 0:4], EPS, None, ALU.add).then_inc(ln2_ve, 1)
                        else:
                            nc.vector.tensor_tensor(xc[:], xc[:], z[0][:, 0:NT], ALU.mult)
                            dve.drain()
                            nc.vector.tensor_copy(x2_hi[:], xc[:])
                            dve.drain()
                            nc.vector.tensor_tensor(x2_lo[:], xc[:], x2_hi[:].bitcast(F32), ALU.subtract).then_inc(x2_done, 1)
                    if body.f and s == 1:
                        softmax(dve, body)
                    if body.f and s == 2:
                        top2(dve, body)
                    if body.f and s >= 10 and (s - 10) % 4 == 0 and (s - 10) // 4 <= NEXP:
                        c = (s - 10) // 4
                        if c == 0:
                            wait(dve, out_stored, body.at(0, f=1) * 16)
                            dve.wait_ge(dn_done, body.at(1, f=9))
                            nc.vector.scalar_tensor_tensor(out=acc[:], in0=dn[:, 0:NT], scalar=sb2_sum[:], in1=h2[:],
                                                           op0=ALU.add, op1=ALU.add).then_inc(comb_done, 1)
                        else:
                            e = c - 1
                            cwb_use = next(k for t in SHARED for k, _, w, g_ in uses(body, t) if (w, g_) == ("cwB", e))
                            dve.wait_ge(sh_free, sh_at(body, cwb_use + 1))
                            wait(dve, acc_done, body.at(e - 1, f=8))
                            dve.wait_ge(dn_done, body.at(c + 1, f=9))
                            nc.vector.tensor_tensor(tmp[e % 2], dn[:, 0:NT], cwB[e % 3], ALU.mult).then_inc(comb_done, 1)
                    for k, khi, what, arg in uses(body, s):
                        dve_shared(dve, body, k, khi, what, arg)

            def pool_body(pool, body, newton):
                for s in range(SLOTS + 1):
                    if body.f and s < BLOCKS:
                        pool.wait_ge(g_hi_done, body.at(s + 1, f=BLOCKS))
                        nc.gpsimd.tensor_tensor(g_lo[s % 3][:], g_raw[s % 2], g_hi[s % 3][:].bitcast(F32),
                                                ALU.subtract).then_inc(g_lo_done, 1)
                    if body.f and s == 2:
                        pool.wait_ge(bigger_done, body.at(1, f=1))
                        nc.gpsimd.tensor_tensor(pairs[:], bigger[:], later[:].unsqueeze(1).broadcast_to([IC, 4, NEXP * NEXP]),
                                                ALU.mult).then_inc(pairs_done, 1)
                    u = scores_at(s - 1)
                    if body.h and u is not None:
                        pool.wait_ge(ntau_done, body.at(u + 1, h=UNITS))
                        nc.gpsimd.tensor_tensor(over[:], cand[u % 2][:, :, 15], ntau[u % 2][:], ALU.add).then_inc(over_done, 1)
                        pool.drain()
                        nc.gpsimd.tensor_scalar(over[:], over[:], 0.0, None, ALU.is_gt)
                        pool.drain()
                        nc.gpsimd.tensor_tensor(worst[:], worst[:], over[:], ALU.add)
                        pool.drain()
                    for _, _, what, _ in uses(body, s):
                        if what == "var":
                            pool.wait_ge(ln1_ve, body.at(1, n=1))
                            nc.gpsimd.tensor_tensor(rs[:], ve[:], mhalf[:], ALU.pow).then_inc(ln1_rs, 1)
                    if body.h and LN2.get(s) == "var":
                        pool.wait_ge(ln2_ve, body.at(1, h=1))
                        nc.gpsimd.tensor_tensor(rs[:], ve[:], mhalf[:], ALU.pow).then_inc(ln2_rs, 1)
                    if body.f and s >= 14 and (s - 14) % 4 == 0 and (s - 14) // 4 < NEXP:
                        e = (s - 14) // 4
                        pool.wait_ge(comb_done, body.at(e + 2, f=9))
                        nc.gpsimd.tensor_tensor(acc[:], acc[:], tmp[e % 2], ALU.add).then_inc(acc_done, 1)

            with nc.Block() as block:
                @block.sync
                def _(sp):
                    bodies(sp, lambda b, nw: sp_body(sp, b, nw), 0, False)
                    sp.wait_ge(out_stored, 16 * G)
                    sp.wait_ge(flag_done, 1)
                    rows = sp.value_load(flag[0:1, 0:1])
                    either(sp, rows, lambda: (bodies(sp, lambda b, nw: sp_body(sp, b, nw), 1, True),
                                              sp.wait_ge(out_stored, 32 * G)))

                @block.scalar
                def _(act):
                    for e in range(NE):
                        if e >= 3:
                            act.wait_ge(w_lo_done, e - 2)
                        act.dma_start(wst[e % 3], ew[e]).then_inc(w_loaded[e % 3], 16)
                        if e >= 2:
                            act.wait_ge(w_loaded[(e - 2) % 3], 16 * ((e - 2) // 3 + 1))
                            nc.scalar.activation(ew_hi[:, (e - 2) * WCH:(e - 1) * WCH], wst[(e - 2) % 3],
                                                 ACT.Copy).then_inc(w_hi_done, 1)
                    for e in (NE - 2, NE - 1):
                        act.wait_ge(w_loaded[e % 3], 16 * (e // 3 + 1))
                        nc.scalar.activation(ew_hi[:, e * WCH:(e + 1) * WCH], wst[e % 3], ACT.Copy).then_inc(w_hi_done, 1)
                    act.wait_ge(ready, 1)
                    act.wait_ge(w_lo_done, NE)
                    bodies(act, lambda b, nw: act_body(act, b, nw), 0, False)
                    act.wait_ge(flag_done, 1)
                    rows = act.value_load(flag[0:1, 0:1])
                    either(act, rows, lambda: bodies(act, lambda b, nw: act_body(act, b, nw), 1, True))

                @block.gpsimd
                def _(pool):
                    for e in range(NE):
                        pool.wait_ge(w_hi_done, e + 1)
                        nc.gpsimd.tensor_tensor(ew_lo[:, e * WCH:(e + 1) * WCH], wst[e % 3],
                                                ew_hi[:, e * WCH:(e + 1) * WCH].bitcast(F32),
                                                ALU.subtract).then_inc(w_lo_done, 1)
                    pool.wait_ge(ready, 1)
                    bodies(pool, lambda b, nw: pool_body(pool, b, nw), 0, False)
                    pool.drain().then_inc(worst_done, 1)
                    pool.wait_ge(flag_done, 1)
                    rows = pool.value_load(flag[0:1, 0:1])
                    either(pool, rows, lambda: bodies(pool, lambda b, nw: pool_body(pool, b, nw), 1, True))

                @block.vector
                def _(dve):
                    nc.vector.memset(at[:], 0.0)
                    for r in range(2):
                        nc.vector.memset(at_hi[r][:, :, T:TP].bitcast(F32), 0.0)
                        nc.vector.memset(at_lo[r][:, :, T:TP].bitcast(F32), 0.0)
                        nc.vector.memset(cand[r][:], 0.0)
                    nc.vector.memset(zero_row[:], 0.0)
                    dve.drain()
                    nc.vector.memset(nrec[:], 1.0).then_inc(ready, 1)
                    bodies(dve, lambda b, nw: dve_body(dve, b, nw), 0, False)
                    dve.wait_ge(worst_done, 1)
                    nc.vector.tensor_scalar(nsum[:], worst[:], 0.0, None, ALU.is_gt)
                    nc.vector.drain().then_inc(flag_sum, 1)
                    dve.wait_ge(flag_sum, 2)
                    nc.vector.tensor_copy(flag[:], sh[0:1, 0:1]).then_inc(flag_done, 1)
                    dve.wait_ge(flag_done, 1)
                    rows = dve.value_load(flag[0:1, 0:1])
                    either(dve, rows, lambda: bodies(dve, lambda b, nw: dve_body(dve, b, nw), 1, True))

                @block.tensor
                def _(pe):
                    pe.wait_ge(ready, 1)
                    pe.wait_ge(w_lo_done, NE)
                    bodies(pe, lambda b, nw: pe_body(pe, b, nw), 0, False)
                    pe.wait_ge(flag_sum, 1)
                    for c in range(2):
                        last = nc.tensor.matmul(sh[0:1, 0:1], nsum[0:NI[c], c:c + 1], mean_w[0:NI[c], 0:1],
                                                start=c == 0, stop=c == 1)
                    last.then_inc(flag_sum, 1)
                    pe.wait_ge(flag_done, 1)
                    rows = pe.value_load(flag[0:1, 0:1])
                    either(pe, rows, lambda: bodies(pe, lambda b, nw: pe_body(pe, b, nw), 1, True))


def kernel(x, L0_tok_W0, L0_tok_b0, L0_tok_pos0, L0_tok_W1, L0_tok_b1, L0_tok_pos1, L0_tok_W2, L0_tok_b2,
           L0_tok_pos2, L0_tok_scale_emb, L0_attn_W_qkv, L0_attn_W_out, L0_attn_b_out, L0_ffn_gate_w,
           L0_ffn_gate_b, L0_ffn_sw1, L0_ffn_sb1, L0_ffn_sw2, L0_ffn_sb2, L0_ffn_rw1, L0_ffn_rb1,
           L0_ffn_rw2, L0_ffn_rb2):
    import numpy as np
    import concourse.bacc as bacc
    from concourse.bass_utils import run_bass_kernel_spmd

    def arr(v):
        return np.asarray(v)

    xt = arr(x).reshape(G, NB, CTX // 4, 4, P).transpose(0, 4, 1, 3, 2)
    xT = np.zeros((G, P, NB, XR, XM), xt.dtype)
    xT[..., :CTX // 4] = xt

    def patch_weights(w, p):
        return arr(w).reshape(P, p, P).transpose(2, 1, 0).reshape(P, p * P)

    def column(v):
        return arr(v).reshape(-1, 1)

    wqkv = arr(L0_attn_W_qkv)
    inner = HEADS * DH
    w1 = np.concatenate([arr(L0_ffn_sw1), arr(L0_ffn_rw1)])
    w2 = np.concatenate([arr(L0_ffn_sw2), arr(L0_ffn_rw2)])
    up_w = w1.transpose(0, 2, 1)
    dn_w = w2.reshape(-1, P, FB, P).transpose(0, 3, 2, 1).reshape(-1, P, FF)
    ins = {
        "xT": xT.reshape(G, P, NB * XB),
        "w0T": patch_weights(L0_tok_W0, PATCH[0]),
        "w1T": patch_weights(L0_tok_W1, PATCH[1]),
        "w2T": patch_weights(L0_tok_W2, PATCH[2]),
        "posT": np.concatenate([arr(v)[0] for v in (L0_tok_pos0, L0_tok_pos1, L0_tok_pos2)]).T,
        "b0": column(L0_tok_b0), "b1": column(L0_tok_b1), "b2": column(L0_tok_b2),
        "seT": arr(L0_tok_scale_emb).T,
        "wqkT": wqkv[:, :2 * inner],
        "wvT": wqkv[:, 2 * inner:].reshape(P, HEADS, DH).transpose(2, 1, 0).reshape(DH, HEADS * P),
        "woutT": arr(L0_attn_W_out).reshape(HEADS, DH, P).transpose(1, 0, 2).reshape(DH, HEADS * P),
        "b_out": column(L0_attn_b_out),
        "gateT": arr(L0_ffn_gate_w).T,
        "gate_b": arr(L0_ffn_gate_b),
        "ew": np.concatenate([up_w, dn_w], axis=2),
        "eb1": np.concatenate([arr(L0_ffn_sb1), arr(L0_ffn_rb1)]).reshape(BLOCKS, P).T,
        "sb2T": arr(L0_ffn_sb2).T,
        "rb2": arr(L0_ffn_rb2),
    }
    nc = bacc.Bacc("TRN2", target_bir_lowering=False, num_devices=1)
    arrays, args = {}, []
    for name, v in ins.items():
        v = np.ascontiguousarray(v)
        arrays[f"in_{name}"] = v
        args.append(nc.dram_tensor(f"in_{name}", v.shape, mybir.dt.from_np(v.dtype), kind="ExternalInput").ap())
    out = nc.dram_tensor("out_T", (G, P, NT), F32, kind="ExternalOutput").ap()
    build(nc, *args, out)
    r = run_bass_kernel_spmd(nc, [arrays], core_ids=[0])
    got = r.results[0]["out_T"].reshape(G, P, NB, TP)[..., :T]
    return np.ascontiguousarray(got.transpose(0, 2, 3, 1).reshape(BATCH, T, P))
```

```python
from contextlib import ExitStack

import concourse.bass as bass
from concourse import mybir

F32 = mybir.dt.float32
F32R = mybir.dt.float32r
I32 = mybir.dt.int32
ACT = mybir.ActivationFunctionType
ALU = mybir.AluOpType
AX = mybir.AxisListType

P = 128
PATCH = (8, 16, 32)
CTX = 512
NTOK = tuple((CTX - p) // (p // 2) + 1 for p in PATCH)
TOFF = (0, NTOK[0], NTOK[0] + NTOK[1])
T = sum(NTOK)
TP = T + 1
NB = 2
NT = NB * TP
IC = TP // 2
NI = (IC, T - IC)
BATCH = 64
G = BATCH // NB
HEADS, DH = 8, 64
HALF = HEADS // 2 * P
NEXP, NSH = 8, 2
FF = 512
FB = FF // P
BLOCKS = (NSH + NEXP) * FB
EPS = 1e-5
NEG = -3.0e38

XR, XM = 4, CTX // 4 + 4
XB = XR * XM
SB = 8
STEPS = BATCH // SB
CW = 2 * XB
WCH = 1024

LAG = 3
SLOTS = BLOCKS + LAG
UNITS = NB * HEADS
NEWTON = 24


def head_of(u):
    return u // 4, (u // 2) % 2, u % 2


def unit_at(s, first):
    return (s - first) // 2 if (s - first) % 2 == 0 and 0 <= (s - first) // 2 < UNITS else None


def scores_at(s):
    return 0 if s == 0 else unit_at(s, -1)


def attention_at(s):
    return unit_at(s, 1)


def transposes_at(s):
    return unit_at(s, 2)


def values_at(s):
    return unit_at(s, 4)


ACT_ROUNDS = (1, 3)
OUT_AT = 35
SHARED = {0: [("logits", 0, "f")], 7: [("cwT", 0, "f")],
          6: [("q", 2, "h")], 8: [("k", 2, "h")], 14: [("q", 3, "h")], 16: [("k", 3, "h")],
          10: [("mean", 0, "n")], 12: [("var", 0, "n")], 18: [("spread", 0, "n")],
          20: [("v", (0, 0, 0), "n")], 22: [("q", 0, "n")], 24: [("v", (0, 1, 0), "n")],
          25: [("k", 0, "n")], 26: [("v", (1, 0, 0), "n")], 28: [("v", (1, 1, 0), "n")],
          30: [("q", 1, "n")], 32: [("k", 1, "n")],
          34: [("v", (0, 0, 1), "n")], 36: [("mean2", 0, "h")], 37: [("v", (0, 1, 1), "n")],
          39: [("v", (1, 0, 1), "n")], 41: [("v", (1, 1, 1), "n")]}
for _e in range(NEXP):
    SHARED.setdefault(9 + 4 * _e, []).append(("cwB", _e, "f"))
SQUARE1_AT, SQUARE2_AT = 11, 37
LN2 = {38: "var", 40: "spread"}
N_SHARED = {k: sum(x[2] == k for v in SHARED.values() for x in v) for k in "fhn"}


class Body:

    def __init__(self, f, h, n, nf, nh, nn, g, i=None):
        self.f, self.h, self.n = f, h, n
        self.nf, self.nh, self.nn = nf, nh, nn
        self.g, self.i = g, i

    def at(self, count, f=0, h=0, n=0):
        static = self.nf * f + self.nh * h + self.nn * n + count
        if self.i is None:
            return static
        return self.i * (f * self.f + h * self.h + n * self.n) + static

    def shared(self):
        k = 0
        for s in sorted(SHARED):
            for what, arg, part in SHARED[s]:
                if getattr_part(self, part):
                    yield s, k, what, arg, part
                    k += 1


def getattr_part(body, part):
    return {"f": body.f, "h": body.h, "n": body.n}[part]


def wait(eng, sem, value):
    if not isinstance(value, int) or value > 0:
        eng.wait_ge(sem, value)


def attention_and_experts(nc, run, newton):
    pass


def build(nc, xT, w0T, w1T, w2T, posT, b0, b1, b2, seT, wqkT, wvT, woutT, b_out,
          gateT, gate_b, ew, eb1, sb2T, rb2, out):
    hs = nc.dram_tensor("h_scratch", (G, P, NT), F32, kind="Internal").ap()

    with ExitStack() as keep:
        def sbuf(name, shape, dt=F32, ctx=keep):
            return ctx.enter_context(nc.sbuf_tensor(name, shape, dt))

        def sem(name):
            return keep.enter_context(nc.semaphore(name))

        banks = [keep.enter_context(nc.psum_tensor(f"bank{i}", [P, 512], F32)) for i in range(8)]

        wqk_hi, wqk_lo = sbuf("wqk_hi", [P, 1024], F32R), sbuf("wqk_lo", [P, 1024], F32R)
        wvo_hi, wvo_lo = sbuf("wvo_hi", [P, 1024], F32R), sbuf("wvo_lo", [P, 1024], F32R)
        gate_hi, gate_lo = sbuf("gate_hi", [P, NEXP], F32R), sbuf("gate_lo", [P, NEXP], F32R)
        gate_raw = sbuf("gate_raw", [P, NEXP])
        rb2_raw = sbuf("rb2_raw", [NEXP, P])
        rb2_hi, rb2_lo = sbuf("rb2_hi", [NEXP, P], F32R), sbuf("rb2_lo", [NEXP, P], F32R)
        gb = sbuf("gb", [P, NEXP])
        bo = sbuf("bo", [P, 1])
        up_bias = sbuf("up_bias", [P, BLOCKS])
        sb2 = sbuf("sb2", [P, NSH])
        sb2_sum = sbuf("sb2_sum", [P, 1])
        ident = sbuf("ident", [P, P])
        id8 = sbuf("id8", [NEXP, NEXP], F32R)
        mean_w = sbuf("mean_w", [P, P])
        later = sbuf("later", [IC, NEXP * NEXP])
        e_index = sbuf("e_index", [IC, 4 * NEXP])
        rinv = sbuf("rinv", [IC, 32])
        seg = sbuf("seg", [IC, 32])
        mhalf = sbuf("mhalf", [IC, 4])
        worst = sbuf("worst", [IC, 2])
        flag = sbuf("flag", [1, 1], I32)

        with ExitStack() as first:
            def sb1(name, shape, dt=F32):
                return sbuf(name, shape, dt, first)

            wcols = (PATCH[0] * P, PATCH[1] * P, PATCH[2] * P)
            w_hi = [sb1(f"w{i}_hi", [P, n], F32R) for i, n in enumerate(wcols)]
            w_lo = [sb1(f"w{i}_lo", [P, n], F32R) for i, n in enumerate(wcols)]
            x_hi = [sb1(f"x_hi{i}", [P, SB * XB], F32R) for i in range(2)]
            x_lo = [sb1(f"x_lo{i}", [P, SB * XB], F32R) for i in range(2)]
            raw = [sb1(f"raw{i}", [P, CW]) for i in range(2)]
            stage = [sb1(f"stage{i}", [P, SB, TP]) for i in range(2)]
            table = sb1("table", [P, T])
            bvec, svec = sb1("bvec", [P, 3]), sb1("svec", [P, 3])
            wv_raw, wo_raw = sb1("wv_raw", [DH, 1024]), sb1("wo_raw", [DH, 1024])

            small = sem("small_loaded")
            memset_done = sem("memset_done")
            raw_loaded = [sem("raw_loaded0"), sem("raw_loaded1")]
            hi_done = sem("hi_done")
            lo_done = sem("lo_done")
            const_done = sem("const_done")
            fold_done = sem("fold_done")
            fold_hi = sem("fold_hi")
            fold_lo = sem("fold_lo")
            emb_done = sem("emb_done")
            emb_out = sem("emb_out")
            h_stored = [sem("h_stored0"), sem("h_stored1")]

            chunks = [("w", 0, 0)] + [("x", 0, q) for q in range(4)] + [("w", 1, 0), ("w", 1, 1)]
            chunks += [("w", 2, q) for q in range(4)] + [("qk", 0, 0)]
            FIRSTC = len(chunks)

            def chunk_no(k, q):
                return q + 1 if isinstance(k, int) and k == 0 else (k - 1) * 4 + FIRSTC + q

            def loads(sp, k, seq):
                for c, par, before, src, n in seq:
                    wait(sp, lo_done, c - 1)
                    sp.dma_start(raw[par][:, 0:n], src).then_inc(raw_loaded[par], 16)

            def x_chunks(k):
                assert FIRSTC % 2 == 0
                for q in range(4):
                    c = chunk_no(k, q)
                    yield c, q % 2, c, (k, q)

            def loaded_value(c, par):
                return (c - par) * 8 + 16

            with nc.Block() as block:
                @block.sync
                def _(sp):
                    sp.dma_start(wv_raw[:], wvT).then_inc(small, 16)
                    sp.dma_start(wo_raw[:], woutT).then_inc(small, 16)
                    for c, (kind, a, q) in enumerate(chunks):
                        wait(sp, lo_done, c - 1)
                        src = {"w": (w0T, w1T, w2T)[a][:, q * WCH:(q + 1) * WCH] if kind == "w" else None,
                               "x": xT[q], "qk": wqkT}[kind]
                        n = CW if kind == "x" else WCH
                        sp.dma_start(raw[c % 2][:, 0:n], src).then_inc(raw_loaded[c % 2], 16)

                    def step(k, par):
                        for q in range(4):
                            c = chunk_no(k + 1, q)
                            sp.wait_ge(lo_done, c - 1)
                            sp.dma_start(raw[q % 2][:, :], xT[(k + 1) * 4 + q]).then_inc(raw_loaded[q % 2], 16)
                        store(k, par)

                    def store(k, par):
                        sp.wait_ge(emb_out, k * 4 + 4)
                        sp.dma_start(hs[bass.ds(k * 4, 4)].rearrange("g p (b t) -> p g b t", b=NB),
                                     stage[par][:].rearrange("p (g b) t -> p g b t", b=NB)).then_inc(h_stored[par], 16)

                    step(0, 0)
                    with sp.Fori(0, (STEPS - 2) // 2) as i:
                        step(i * 2 + 1, 1)
                        step(i * 2 + 2, 0)
                    store(STEPS - 1, 1)
                    for par in range(2):
                        sp.wait_ge(h_stored[par], 16 * STEPS // 2)

                @block.gpsimd
                def _(pool):
                    nc.gpsimd.memset(ident[:], 0.0)
                    nc.gpsimd.memset(later[:], 0.0)
                    nc.gpsimd.memset(mean_w[:], 1.0 / P)
                    nc.gpsimd.memset(seg[:], 1.0)
                    nc.gpsimd.memset(mhalf[:], -0.5)
                    nc.gpsimd.memset(worst[:], 0.0)
                    for r in range(16):
                        nc.gpsimd.memset(rinv[:, r:r + 17:16], 1.0 / (r + 1))
                    for e in range(NEXP):
                        nc.gpsimd.memset(e_index[:, e:e + 3 * NEXP + 1:NEXP], float(e))
                    for par in range(2):
                        nc.gpsimd.memset(stage[par][:, :, T:TP], 0.0)
                    pool.drain()
                    nc.gpsimd.memset(seg[:, 0:17:16], 0.0)
                    for first_e in range(1, NEXP):
                        nc.gpsimd.memset(later[:, first_e * NEXP:first_e * NEXP + first_e], 1.0)
                    nc.gpsimd.affine_select(out=ident[:], in_=ident[:], compare_op=ALU.not_equal, fill=1.0,
                                            base=0, pattern=[[-1, P]], channel_multiplier=1)
                    pool.drain()
                    nc.gpsimd.memset(flag[:], 0).then_inc(memset_done, 1)

                @block.scalar
                def _(act):
                    for dst, src in ((gate_raw, gateT), (rb2_raw, rb2), (bo, b_out), (up_bias, eb1),
                                     (sb2, sb2T), (table, posT), (svec, seT)):
                        act.dma_start(dst[:], src).then_inc(small, 16)
                    for s, b in enumerate((b0, b1, b2)):
                        act.dma_start(bvec[:, s:s + 1], b).then_inc(small, 16)
                    act.dma_start(gb[:], gate_b.partition_broadcast(P)).then_inc(small, 16)
                    for half in range(2):
                        act.wait_ge(fold_done, half + 1)
                        nc.scalar.activation(wvo_hi[:, half * HALF:(half + 1) * HALF], banks[half][:],
                                             ACT.Copy).then_inc(fold_hi, 1)
                    for c, (kind, a, q) in enumerate(chunks):
                        act.wait_ge(raw_loaded[c % 2], loaded_value(c, c % 2))
                        dst = (x_hi[0][:, q * CW:(q + 1) * CW] if kind == "x" else wqk_hi[:] if kind == "qk"
                               else w_hi[a][:, q * WCH:(q + 1) * WCH])
                        n = CW if kind == "x" else WCH
                        nc.scalar.activation(dst, raw[c % 2][:, 0:n], ACT.Copy).then_inc(hi_done, 1)

                    def step(k, par):
                        if not isinstance(k, int) or k >= 2:
                            act.wait_ge(emb_done, k * 4 - 4)
                        for q in range(4):
                            c = chunk_no(k, q)
                            act.wait_ge(raw_loaded[q % 2], loaded_value(c, q % 2))
                            nc.scalar.activation(x_hi[par][:, q * CW:(q + 1) * CW], raw[q % 2][:],
                                                 ACT.Copy).then_inc(hi_done, 1)

                    step(1, 1)
                    with act.Fori(0, (STEPS - 2) // 2) as i:
                        step(i * 2 + 2, 0)
                        step(i * 2 + 3, 1)

                @block.vector
                def _(dve):
                    for half in range(2):
                        cols = slice(half * HALF, (half + 1) * HALF)
                        dve.wait_ge(fold_hi, half + 1)
                        nc.vector.tensor_tensor(wvo_lo[:, cols], banks[half][:], wvo_hi[:, cols].bitcast(F32),
                                                ALU.subtract).then_inc(fold_lo, 1)
                    dve.wait_ge(small, 13 * 16)
                    dve.wait_ge(memset_done, 1)
                    nc.vector.tensor_copy(gate_hi[:], gate_raw[:])
                    nc.vector.tensor_copy(rb2_hi[:], rb2_raw[:])
                    nc.vector.tensor_copy(id8[:], ident[0:NEXP, 0:NEXP])
                    nc.vector.tensor_tensor(bvec[:], bvec[:], svec[:], ALU.add)
                    nc.vector.tensor_tensor(sb2_sum[:], sb2[:, 0:1], sb2[:, 1:2], ALU.add)
                    dve.drain()
                    nc.vector.tensor_tensor(gate_lo[:], gate_raw[:], gate_hi[:].bitcast(F32), ALU.subtract)
                    nc.vector.tensor_tensor(rb2_lo[:], rb2_raw[:], rb2_hi[:].bitcast(F32), ALU.subtract)
                    for s in range(3):
                        cols = slice(TOFF[s], TOFF[s] + NTOK[s])
                        nc.vector.tensor_scalar(table[:, cols], table[:, cols], bvec[:, s:s + 1], None, ALU.add)
                    dve.drain()
                    for c, (kind, a, q) in enumerate(chunks):
                        dst, hi = ((x_lo[0][:, q * CW:(q + 1) * CW], x_hi[0][:, q * CW:(q + 1) * CW]) if kind == "x" else
                                   (wqk_lo[:], wqk_hi[:]) if kind == "qk" else
                                   (w_lo[a][:, q * WCH:(q + 1) * WCH], w_hi[a][:, q * WCH:(q + 1) * WCH]))
                        n = CW if kind == "x" else WCH
                        dve.wait_ge(hi_done, c + 1)
                        nc.vector.tensor_tensor(dst, raw[c % 2][:, 0:n], hi.bitcast(F32),
                                                ALU.subtract).then_inc(lo_done, 1)

                    def low(k, par):
                        for q in range(4):
                            dve.wait_ge(hi_done, chunk_no(k, q) + 1)
                            cols = slice(q * CW, (q + 1) * CW)
                            nc.vector.tensor_tensor(x_lo[par][:, cols], raw[q % 2][:], x_hi[par][:, cols].bitcast(F32),
                                                    ALU.subtract).then_inc(lo_done, 1)

                    def bank_out(k, par, use, dst_b, nb, s, width):
                        n, off = NTOK[s], TOFF[s]
                        dve.wait_ge(emb_done, k * 4 + use + 1)
                        src = banks[par * 4 + use][:, 0:nb * width].rearrange("p (b t) -> p b t", b=nb)[:, :, 0:n]
                        add = table[:, off:off + n].unsqueeze(1).broadcast_to([P, nb, n])
                        nc.vector.tensor_tensor(stage[par][:, dst_b:dst_b + nb, off:off + n], src, add,
                                                ALU.add).then_inc(emb_out, 1)

                    def outs(k, par, wait_store):
                        if wait_store is not None:
                            dve.wait_ge(h_stored[par], wait_store)
                        bank_out(k, par, 0, 0, 4, 0, NTOK[0] + 1)
                        bank_out(k, par, 1, 4, 4, 0, NTOK[0] + 1)
                        bank_out(k, par, 2, 0, SB, 1, NTOK[1] + 1)
                        bank_out(k, par, 3, 0, SB, 2, NTOK[2] + 1)

                    low(1, 1)
                    outs(0, 0, None)
                    low(2, 0)
                    outs(1, 1, None)
                    with dve.Fori(0, (STEPS - 4) // 2) as i:
                        low(i * 2 + 3, 1)
                        outs(i * 2 + 2, 0, i * 16 + 16)
                        low(i * 2 + 4, 0)
                        outs(i * 2 + 3, 1, i * 16 + 16)
                    low(STEPS - 1, 1)
                    outs(STEPS - 2, 0, (STEPS // 2 - 1) * 16)
                    outs(STEPS - 1, 1, (STEPS // 2 - 1) * 16)

                @block.tensor
                def _(pe):
                    pe.wait_ge(small, 13 * 16)
                    for half in range(2):
                        for j in range(HEADS // 2):
                            h = half * HEADS // 2 + j
                            last = nc.tensor.matmul(banks[half][:, j * P:(j + 1) * P], wv_raw[:, h * P:(h + 1) * P],
                                                    wo_raw[:, h * P:(h + 1) * P], start=True, stop=True)
                        last.then_inc(fold_done, 1)

                    def products(out_ap, s, j, par, b0_, nb, n, first_, last_):
                        st = PATCH[s] // 8
                        def moving(x):
                            v = x[par][:].rearrange("p (b r m) -> p b r m", b=SB, r=XR)
                            return v[:, b0_:b0_ + nb, j % XR, j // XR:j // XR + st * (n - 1) + 1:st]
                        cols = slice(j * P, (j + 1) * P)
                        nc.tensor.matmul(out_ap, w_hi[s][:, cols], moving(x_hi), start=first_, stop=False)
                        nc.tensor.matmul(out_ap, w_hi[s][:, cols], moving(x_lo), start=False, stop=False)
                        return nc.tensor.matmul(out_ap, w_lo[s][:, cols], moving(x_hi), start=False, stop=last_)

                    def step(k, par, cold=False):
                        if not isinstance(k, int) or k >= 2:
                            pe.wait_ge(emb_out, k * 4 - 4)
                        if cold:
                            pe.wait_ge(fold_lo, 2)
                        for use, s, b0_, nb in ((0, 0, 0, 4), (1, 0, 4, 4), (2, 1, 0, SB), (3, 2, 0, SB)):
                            n = NTOK[s] + 1
                            if use < 2:
                                pe.wait_ge(lo_done, chunk_no(k, 2 * use + 1) + 1)
                            elif cold:
                                pe.wait_ge(lo_done, 7 if s == 1 else 11)
                            o = banks[par * 4 + use][:, 0:nb * n]
                            for j in range(PATCH[s]):
                                last = products(o, s, j, par, b0_, nb, n, j == 0, j == PATCH[s] - 1)
                            last.then_inc(emb_done, 1)

                    step(0, 0, True)
                    step(1, 1)
                    with pe.Fori(0, (STEPS - 2) // 2) as i:
                        step(i * 2 + 2, 0)
                        step(i * 2 + 3, 1)

        with ExitStack() as second:
            def sb2_(name, shape, dt=F32):
                return sbuf(name, shape, dt, second)

            NE = (NSH + NEXP)
            ew_hi, ew_lo = sb2_("ew_hi", [P, NE * WCH], F32R), sb2_("ew_lo", [P, NE * WCH], F32R)
            rings = sb2_("rings", [P, 6 * NT])
            cwB = [rings[:, i * NT:(i + 1) * NT] for i in range(2)]
            g_raw = [rings[:, (2 + i) * NT:(3 + i) * NT] for i in range(2)]
            tmp = [rings[:, (4 + i) * NT:(5 + i) * NT] for i in range(2)]
            wst = [rings[:, i * WCH:(i + 1) * WCH] for i in range(2)]
            x1_hi, x1_lo = sb2_("x1_hi", [P, NT], F32R), sb2_("x1_lo", [P, NT], F32R)
            x2_hi, x2_lo = sb2_("x2_hi", [P, NT], F32R), sb2_("x2_lo", [P, NT], F32R)
            qk_hi = {(w, r): sb2_(f"{w}_hi{r}", [P, NT], F32R) for w in "qk" for r in range(2)}
            qk_lo = {(w, r): sb2_(f"{w}_lo{r}", [P, NT], F32R) for w in "qk" for r in range(2)}
            v_hi = sb2_("v_hi", [IC, NB, 2, 2 * HALF], F32R)
            v_lo = sb2_("v_lo", [IC, NB, 2, 2 * HALF], F32R)
            a = [sb2_(f"a{r}", [IC, 2, TP]) for r in range(2)]
            at_hi = [sb2_(f"at_hi{r}", [IC, 2, TP], F32R) for r in range(2)]
            at_lo = [sb2_(f"at_lo{r}", [IC, 2, TP], F32R) for r in range(2)]
            g_hi = [sb2_(f"g_hi{r}", [P, NT], F32R) for r in range(4)]
            g_lo = [sb2_(f"g_lo{r}", [P, NT], F32R) for r in range(4)]
            h_next, h_res, h2, acc = (sb2_(n, [P, NT]) for n in ("h_next", "h_res", "h2", "acc"))
            xc, sq = sb2_("xc", [P, NT]), sb2_("sq", [P, NT])
            cwT_hi, cwT_lo = sb2_("cwT_hi", [NEXP, NT], F32R), sb2_("cwT_lo", [NEXP, NT], F32R)
            z_rest = [sb2_(f"z_rest{i}", [IC, T]) for i in range(2)]
            cand = [sb2_(f"cand{r}", [IC, 2, 16]) for r in range(2)]
            sums, taus = sb2_("sums", [IC, 32]), sb2_("taus", [IC, 32])
            ntau = [sb2_(f"ntau{r}", [IC, 2]) for r in range(2)]
            over = sb2_("over", [IC, 2])
            ve, rs = sb2_("ve", [IC, 4]), sb2_("rs", [IC, 4])
            lg, ex, pr, cw = (sb2_(n, [IC, 4, NEXP]) for n in ("lg", "ex", "pr", "cw"))
            lmax, lsum, lrec = (sb2_(n, [IC, 4]) for n in ("lmax", "lsum", "lrec"))
            bigger = sb2_("bigger", [IC, 4, NEXP * NEXP])
            pairs = sb2_("pairs", [IC, 4, NEXP * NEXP])
            s_col, s_row, rank = (sb2_(n, [IC, 4, NEXP]) for n in ("s_col", "s_row", "rank"))
            nsum, ncnt, nrec = (sb2_(n, [IC, 2]) for n in ("nsum", "ncnt", "nrec"))

            z = banks[0:2]
            at = banks[2]
            y = banks[3]
            shb = banks[4:6]
            up = banks[6]
            dn = banks[7]

            ready = sem("ready")
            w_loaded = [sem(f"w_loaded{i}") for i in range(2)]
            w_hi_done = sem("w_hi_done")
            w_lo_done = sem("w_lo_done")
            next_loaded = sem("next_loaded")
            res_loaded = sem("res_loaded")
            out_stored = sem("out_stored")
            sh_done = sem("sh_done")
            sh_hi = sem("sh_hi")
            sh_free = [sem("sh_free0"), sem("sh_free1")]
            ln1_xc, ln2_xc = sem("ln1_xc"), sem("ln2_xc")
            ln1_sq, ln2_sq = sem("ln1_sq"), sem("ln2_sq")
            ln1_ve, ln2_ve = sem("ln1_ve"), sem("ln2_ve")
            ln1_rs, ln2_rs = sem("ln1_rs"), sem("ln2_rs")
            x1_done, x2_done = sem("x1_done"), sem("x2_done")
            ln2_pe = sem("ln2_pe")
            z_done = sem("z_done")
            z_read = sem("z_read")
            ntau_done = sem("ntau_done")
            over_done = sem("over_done")
            relu_done = sem("relu_done")
            at_done = sem("at_done")
            at_hi_done = sem("at_hi_done")
            at_lo_done = sem("at_lo_done")
            y_done = sem("y_done")
            h2_done = sem("h2_done")
            up_done = sem("up_done")
            gelu_done = sem("gelu_done")
            g_hi_act, g_hi_dve = sem("g_hi_act"), sem("g_hi_dve")
            g_lo_done = sem("g_lo_done")
            dn_done = sem("dn_done")
            comb_done = sem("comb_done")
            acc_done = sem("acc_done")
            lg_done = sem("lg_done")
            ex_done = sem("ex_done")
            bigger_done = sem("bigger_done")
            pairs_done = sem("pairs_done")
            cw_done = sem("cw_done")
            flag_sum = sem("flag_sum")
            flag_done = sem("flag_done")
            worst_done = sem("worst_done")

            HAS_HI = ("q", "k", "v", "cwT")

            def hi_uses(body):
                n = {p: sum(x[2] == p and x[0] in HAS_HI for v in SHARED.values() for x in v) for p in "fhn"}
                return n

            N_HI = hi_uses(None)

            def sh_at(body, n):
                return body.at(n, f=N_SHARED["f"], h=N_SHARED["h"], n=N_SHARED["n"])

            def sh_bank(body, k):
                assert body.i is None or sum(N_SHARED.values()) % 2 == 0
                return (body.nf * N_SHARED["f"] + body.nh * N_SHARED["h"] + body.nn * N_SHARED["n"] + k) % 2

            def sh_turn(body, k):
                static = body.nf * N_SHARED["f"] + body.nh * N_SHARED["h"] + body.nn * N_SHARED["n"] + k
                return static // 2 if body.i is None else body.i * (sum(N_SHARED.values()) // 2) + static // 2

            def wait_read(eng, body, k):
                eng.wait_ge(sh_free[sh_bank(body, k)], sh_turn(body, k) + 1)

            def sh_hi_at(body, n):
                return body.at(n, f=N_HI["f"], h=N_HI["h"], n=N_HI["n"])

            def uses(body, s):
                k = khi = 0
                found = []
                for t in sorted(SHARED):
                    for what, arg, part in SHARED[t]:
                        if {"f": body.f, "h": body.h, "n": body.n}[part]:
                            if t == s:
                                found.append((k, khi, what, arg))
                            k += 1
                            khi += what in HAS_HI
                return found

            def use_of(body, what, arg):
                return next(k for t in SHARED for k, _, w, a_ in uses(body, t) if (w, a_) == (what, arg))

            def bodies(eng, emit, base, newton):
                nb = base * G
                emit(Body(0, 0, 1, nb, nb, nb, -1), newton)
                emit(Body(0, 1, 1, nb, nb, nb + 1, 0), newton)
                emit(Body(1, 1, 1, nb, nb + 1, nb + 2, 1), newton)
                with eng.Fori(0, G - 3) as i:
                    emit(Body(1, 1, 1, nb + 1, nb + 2, nb + 3, i + 2, i), newton)
                emit(Body(1, 1, 0, nb + G - 2, nb + G - 1, nb + G, G - 1), newton)
                emit(Body(1, 0, 0, nb + G - 1, nb + G, nb + G, G), newton)

            def act_rounds(s):
                return s % 4 in ACT_ROUNDS

            def g_hi_ready(body, s):
                before = sum(act_rounds(t) == act_rounds(s) for t in range(s + 1))
                total = sum(act_rounds(t) == act_rounds(s) for t in range(BLOCKS))
                return (g_hi_act if act_rounds(s) else g_hi_dve), body.at(before, f=total)

            def loads_weights(body):
                return isinstance(body.nh, int) and body.nh == 0 and body.h

            def either(eng, flag_reg, general):
                with eng.If(flag_reg > 0):
                    general()
                with eng.Else():
                    eng.nop()

            def sp_body(sp, body, newton):
                if body.n:
                    wait(sp, ln1_xc, body.at(0, n=1))
                    sp.dma_start(h_next[:], hs[body.g + 1]).then_inc(next_loaded, 16)
                if body.h:
                    wait(sp, h2_done, body.at(0, h=1))
                    sp.dma_start(h_res[:], hs[body.g]).then_inc(res_loaded, 16)
                if loads_weights(body):
                    for e in range(NE):
                        wait(sp, w_lo_done, e - 1)
                        sp.dma_start(wst[e % 2], ew[e]).then_inc(w_loaded[e % 2], 16)
                if body.f:
                    sp.wait_ge(acc_done, body.at(8, f=8))
                    sp.dma_start(out[body.g - 1], acc[:]).then_inc(out_stored, 16)

            def three(out_ap, s_hi, s_lo, m_hi, m_lo, start=True, stop=True, share=False):
                kw = {"skip_group_check": True} if share else {}
                nc.tensor.matmul(out_ap, s_hi, m_hi, start=start, stop=False, **kw)
                nc.tensor.matmul(out_ap, s_hi, m_lo, start=False, stop=False, **kw)
                return nc.tensor.matmul(out_ap, s_lo, m_hi, start=False, stop=stop, **kw)

            def ln_product(pe, bank, what, src):
                if what == "mean":
                    return nc.tensor.matmul(bank[:, 0:NT], mean_w[:], src[:], start=True, stop=True)
                for c in range(4):
                    cols = slice(c * IC, (c + 1) * IC)
                    if what == "var":
                        last = nc.tensor.matmul(bank[0:IC, c:c + 1], sq[:, cols], mean_w[:, 0:1],
                                                start=True, stop=True)
                    else:
                        last = nc.tensor.matmul(bank[:, cols], rs[:, c:c + 1].broadcast_to([IC, P]),
                                                ident[0:IC, 0:IC], start=True, stop=True)
                return last

            def pe_shared(pe, body, k, what, arg):
                sh = shb[sh_bank(body, k)]
                wait(pe, sh_free[sh_bank(body, k)], sh_turn(body, k))
                source = None
                if what == "cwB":
                    source = use_of(body, "cwT", 0)
                elif what in ("q", "k", "v") and body.n and k > use_of(body, "spread", 0):
                    source = use_of(body, "spread", 0)
                if source is not None and sh_bank(body, source) != sh_bank(body, k):
                    wait_read(pe, body, source)
                if what == "logits":
                    pe.wait_ge(x2_done, body.at(1, f=1))
                    for c in range(4):
                        cols = slice(c * IC, (c + 1) * IC)
                        last = three(sh[0:IC, c * NEXP:(c + 1) * NEXP], x2_hi[:, cols], x2_lo[:, cols],
                                     gate_hi[:], gate_lo[:])
                elif what == "cwT":
                    pe.wait_ge(cw_done, body.at(1, f=1))
                    for c in range(4):
                        last = nc.tensor.transpose(sh[0:NEXP, c * IC:(c + 1) * IC], cw[:, c, :], ident[0:IC, 0:IC])
                elif what == "cwB":
                    sel = id8[:, arg:arg + 1].broadcast_to([NEXP, P])
                    nc.tensor.matmul(sh[:, 0:NT], sel, cwT_hi[:], start=True, stop=False)
                    last = nc.tensor.matmul(sh[:, 0:NT], sel, cwT_lo[:], start=False, stop=True)
                elif what in "qk":
                    cols = slice((what == "k") * 512 + arg * P, (what == "k") * 512 + (arg + 1) * P)
                    last = three(sh[:, 0:NT], wqk_hi[:, cols], wqk_lo[:, cols], x1_hi[:], x1_lo[:])
                elif what == "v":
                    b, c, half = arg
                    rows = slice(b * TP + c * IC, b * TP + (c + 1) * IC)
                    cols = slice(half * HALF, (half + 1) * HALF)
                    last = three(sh[0:IC, :], x1_hi[:, rows], x1_lo[:, rows], wvo_hi[:, cols], wvo_lo[:, cols])
                elif what == "mean2":
                    pe.wait_ge(h2_done, body.at(1, h=1))
                    last = ln_product(pe, sh, "mean", h2)
                else:
                    if what == "mean":
                        pe.wait_ge(next_loaded, body.at(1, n=1) * 16)
                    elif what == "var":
                        pe.wait_ge(ln1_sq, body.at(1, n=1))
                    else:
                        pe.wait_ge(ln1_rs, body.at(1, n=1))
                    last = ln_product(pe, sh, what, h_next)
                last.then_inc(sh_done, 1)

            def pe_body(pe, body, newton):
                for s in range(SLOTS):
                    if body.f and s < BLOCKS:
                        e, fb = divmod(s, FB)
                        cols = slice(e * WCH + fb * P, e * WCH + (fb + 1) * P)
                        if s == 0:
                            pe.wait_ge(x2_done, body.at(1, f=1))
                            if body.i is None and body.nf == 0:
                                pe.wait_ge(w_lo_done, NE)
                        wait(pe, gelu_done, body.at(s, f=BLOCKS))
                        three(up[:, 0:NT], ew_hi[:, cols], ew_lo[:, cols], x2_hi[:], x2_lo[:]).then_inc(up_done, 1)
                    u = scores_at(s)
                    if body.h and u is not None:
                        p, b, j = head_of(u)
                        r, rows = p % 2, slice(j * DH, (j + 1) * DH)
                        wait(pe, relu_done, body.at(u - 1, h=UNITS))
                        if u == 0:
                            wait(pe, x2_done, body.at(0, h=1))
                        if p >= 2:
                            kq, kk = use_of(body, "q", p), use_of(body, "k", p)
                            wait_read(pe, body, kk)
                            if sh_bank(body, kq) != sh_bank(body, kk):
                                wait_read(pe, body, kq)
                        for c in range(2):
                            q0 = b * TP + c * IC
                            last = three(z[u % 2][0:NI[c], c * TP:(c + 1) * TP],
                                         qk_hi["q", r][rows, q0:q0 + NI[c]], qk_lo["q", r][rows, q0:q0 + NI[c]],
                                         qk_hi["k", r][rows, b * TP:(b + 1) * TP], qk_lo["k", r][rows, b * TP:(b + 1) * TP])
                        last.then_inc(z_done, 1)
                    if body.f and 0 <= s - LAG < BLOCKS:
                        d = s - LAG
                        e, fb = divmod(d, FB)
                        cols = slice(e * WCH + 512 + fb * P, e * WCH + 512 + (fb + 1) * P)
                        if (d % FB == 0 and e != 1):
                            wait(pe, comb_done, body.at(max(e - 1, 0), f=9))
                        pe.wait_ge(g_lo_done, body.at(d + 1, f=BLOCKS))
                        last = three(dn[:, 0:NT], ew_hi[:, cols], ew_lo[:, cols], g_hi[d % 4][:], g_lo[d % 4][:],
                                     start=fb == 0 and e != 1, stop=fb == FB - 1 and e > 1)
                        if e == 1 and fb == FB - 1:
                            wait_read(pe, body, use_of(body, "cwT", 0))
                            last = three(dn[:, 0:NT], rb2_hi[:], rb2_lo[:], cwT_hi[:], cwT_lo[:], start=False)
                        if fb == FB - 1 and e >= 1:
                            last.then_inc(dn_done, 1)
                    u = transposes_at(s)
                    if body.h and u is not None:
                        wait(pe, at_lo_done, body.at(u, h=UNITS))
                        pe.wait_ge(relu_done, body.at(u + 1, h=UNITS))
                        for jc in range(2):
                            for c in range(2):
                                last = nc.tensor.transpose(
                                    at[0:NI[jc], jc * TP + c * IC:jc * TP + c * IC + NI[c]],
                                    a[u % 2][0:NI[c], c, jc * IC:jc * IC + NI[jc]], ident[0:NI[c], 0:NI[c]])
                        last.then_inc(at_done, 1)
                    u = values_at(s)
                    if body.h and u is not None:
                        p, b, j = head_of(u)
                        cols = slice((2 * p + j) * P, (2 * p + j + 1) * P)
                        pe.wait_ge(at_lo_done, body.at(u + 1, h=UNITS))
                        if u == 0:
                            wait(pe, h2_done, body.at(0, h=1))
                        for jc in range(2):
                            n = NI[jc]
                            last = three(y[:, b * TP:(b + 1) * TP], v_hi[0:n, b, jc, cols], v_lo[0:n, b, jc, cols],
                                         at_hi[u % 2][0:n, jc, :], at_lo[u % 2][0:n, jc, :],
                                         start=u == 0 and jc == 0, stop=p == 3 and j == 1 and jc == 1, share=True)
                        if u == UNITS - 1:
                            last.then_inc(y_done, 1)
                    if body.h and s in LN2:
                        what = LN2[s]
                        if what == "var":
                            pe.wait_ge(ln2_sq, body.at(1, h=1))
                        else:
                            pe.wait_ge(ln2_rs, body.at(1, h=1))
                        ln_product(pe, z[0], what, h2).then_inc(ln2_pe, 1)
                    for k, _, what, arg in uses(body, s):
                        pe_shared(pe, body, k, what, arg)

            def act_shared(act, body, k, khi, what, arg):
                sh = shb[sh_bank(body, k)]
                if what in HAS_HI:
                    act.wait_ge(sh_done, sh_at(body, k + 1))
                    if what == "v":
                        b, c, half = arg
                        dst, src = v_hi[:, b, c, half * HALF:(half + 1) * HALF], sh[0:IC, :]
                    elif what == "cwT":
                        dst, src = cwT_hi[:], sh[0:NEXP, 0:NT]
                    else:
                        dst, src = qk_hi[what, arg % 2][:], sh[:, 0:NT]
                    nc.scalar.activation(dst, src, ACT.Copy,
                                         scale=DH ** -0.5 if what == "q" else 1.0).then_inc(sh_hi, 1)
                elif what == "cwB":
                    wait(act, comb_done, body.at(arg, f=9))
                    act.wait_ge(sh_done, sh_at(body, k + 1))
                    nc.scalar.activation(cwB[arg % 2], sh[:, 0:NT], ACT.Copy).then_inc(sh_free[sh_bank(body, k)], 1)

            def act_body(act, body, newton):
                for s in range(SLOTS):
                    if loads_weights(body) and s % 4 == 3 and s // 4 < NE:
                        act_weights(act, s // 4)
                    if body.f and s < BLOCKS:
                        wait(act, g_lo_done, body.at(s - 1, f=BLOCKS))
                        act.wait_ge(up_done, body.at(s + 1, f=BLOCKS))
                        nc.scalar.activation(g_raw[s % 2], up[:, 0:NT], ACT.Gelu,
                                             bias=up_bias[:, s:s + 1]).then_inc(gelu_done, 1)
                    if body.f and s == 2:
                        act.wait_ge(lg_done, body.at(1, f=1))
                        nc.scalar.activation(ex[:], lg[:], ACT.Exp).then_inc(ex_done, 1)
                    u = attention_at(s)
                    if body.h and u is not None:
                        act.wait_ge(ntau_done, body.at(u + 1, h=UNITS))
                        for c in range(2):
                            last = nc.scalar.activation(a[u % 2][0:NI[c], c, 0:T], z[u % 2][0:NI[c], c * TP:c * TP + T],
                                                        ACT.Relu, bias=ntau[u % 2][0:NI[c], c:c + 1])
                        last.then_inc(relu_done, 1)
                    if body.f and s < BLOCKS and act_rounds(s):
                        act.wait_ge(gelu_done, body.at(s + 1, f=BLOCKS))
                        nc.scalar.activation(g_hi[s % 4][:], g_raw[s % 2], ACT.Copy).then_inc(g_hi_act, 1)
                    u = transposes_at(s)
                    if body.h and u is not None:
                        act.wait_ge(at_done, body.at(u + 1, h=UNITS))
                        nc.scalar.activation(at_hi[u % 2][:, :, 0:T], at[0:IC, 0:NT].rearrange("p (c t) -> p c t", c=2)[:, :, 0:T],
                                             ACT.Copy).then_inc(at_hi_done, 1)
                    if body.n and s == SQUARE1_AT:
                        act.wait_ge(ln1_xc, body.at(1, n=1))
                        nc.scalar.activation(sq[:], xc[:], ACT.Square).then_inc(ln1_sq, 1)
                    if body.h and s == SQUARE2_AT:
                        act.wait_ge(ln2_xc, body.at(1, h=1))
                        nc.scalar.activation(sq[:], xc[:], ACT.Square).then_inc(ln2_sq, 1)
                    for k, khi, what, arg in uses(body, s):
                        act_shared(act, body, k, khi, what, arg)

            def act_weights(act, e):
                act.wait_ge(w_loaded[e % 2], 16 * (e // 2 + 1))
                nc.scalar.activation(ew_hi[:, e * WCH:(e + 1) * WCH], wst[e % 2], ACT.Copy).then_inc(w_hi_done, 1)

            def pool_weights(pool, e):
                pool.wait_ge(w_hi_done, e + 1)
                nc.gpsimd.tensor_tensor(ew_lo[:, e * WCH:(e + 1) * WCH], wst[e % 2],
                                        ew_hi[:, e * WCH:(e + 1) * WCH].bitcast(F32),
                                        ALU.subtract).then_inc(w_lo_done, 1)

            def dve_shared(dve, body, k, khi, what, arg):
                sh = shb[sh_bank(body, k)]
                done = sh_at(body, k + 1)
                if what in HAS_HI:
                    dve.wait_ge(sh_hi, sh_hi_at(body, khi + 1))
                    if what == "v":
                        b, c, half = arg
                        cols = slice(half * HALF, (half + 1) * HALF)
                        nc.vector.tensor_tensor(v_lo[:, b, c, cols], sh[0:IC, :], v_hi[:, b, c, cols].bitcast(F32),
                                                ALU.subtract).then_inc(sh_free[sh_bank(body, k)], 1)
                    elif what == "q":
                        nc.vector.scalar_tensor_tensor(
                            out=qk_lo["q", arg % 2][:], in0=sh[:, 0:NT], scalar=DH ** -0.5,
                            in1=qk_hi["q", arg % 2][:].bitcast(F32), op0=ALU.mult, op1=ALU.subtract).then_inc(sh_free[sh_bank(body, k)], 1)
                    elif what == "k":
                        nc.vector.tensor_tensor(qk_lo["k", arg % 2][:], sh[:, 0:NT], qk_hi["k", arg % 2][:].bitcast(F32),
                                                ALU.subtract).then_inc(sh_free[sh_bank(body, k)], 1)
                    else:
                        nc.vector.tensor_tensor(cwT_lo[:], sh[0:NEXP, 0:NT], cwT_hi[:].bitcast(F32),
                                                ALU.subtract).then_inc(sh_free[sh_bank(body, k)], 1)
                elif what == "logits":
                    dve.wait_ge(sh_done, done)
                    nc.vector.tensor_tensor(lg[:], sh[0:IC, 0:4 * NEXP].rearrange("p (c e) -> p c e", c=4),
                                            gb[0:IC, :].unsqueeze(1).broadcast_to([IC, 4, NEXP]),
                                            ALU.add).then_inc(sh_free[sh_bank(body, k)], 1)
                    dve.drain()
                    nc.vector.tensor_reduce(lmax[:], lg[:], AX.X, ALU.max)
                    dve.drain()
                    nc.vector.tensor_tensor(lg[:], lg[:], lmax[:].unsqueeze(2).broadcast_to([IC, 4, NEXP]),
                                            ALU.subtract).then_inc(lg_done, 1)
                elif what == "mean":
                    dve.wait_ge(sh_done, done)
                    nc.vector.tensor_tensor(xc[:], h_next[:], sh[:, 0:NT], ALU.subtract).then_inc(ln1_xc, 1)
                    nc.vector.drain().then_inc(sh_free[sh_bank(body, k)], 1)
                elif what == "mean2":
                    dve.wait_ge(sh_done, done)
                    nc.vector.tensor_tensor(xc[:], h2[:], sh[:, 0:NT], ALU.subtract).then_inc(ln2_xc, 1)
                    nc.vector.drain().then_inc(sh_free[sh_bank(body, k)], 1)
                elif what == "var":
                    dve.wait_ge(sh_done, done)
                    nc.vector.tensor_scalar(ve[:], sh[0:IC, 0:4], EPS, None, ALU.add).then_inc(ln1_ve, 1)
                    nc.vector.drain().then_inc(sh_free[sh_bank(body, k)], 1)
                elif what == "spread":
                    dve.wait_ge(sh_done, done)
                    nc.vector.tensor_tensor(xc[:], xc[:], sh[:, 0:NT], ALU.mult)
                    dve.drain()
                    nc.vector.tensor_copy(x1_hi[:], xc[:])
                    dve.drain()
                    nc.vector.tensor_tensor(x1_lo[:], xc[:], x1_hi[:].bitcast(F32), ALU.subtract).then_inc(sh_free[sh_bank(body, k)], 1)

            def softmax(dve, body):
                dve.wait_ge(ex_done, body.at(1, f=1))
                nc.vector.tensor_reduce(lsum[:], ex[:], AX.X, ALU.add)
                dve.drain()
                nc.vector.reciprocal(lrec[:], lsum[:])
                dve.drain()
                nc.vector.tensor_tensor(pr[:], ex[:], lrec[:].unsqueeze(2).broadcast_to([IC, 4, NEXP]),
                                        ALU.mult)
                dve.drain()
                nc.vector.tensor_tensor(bigger[:].rearrange("p c (i e) -> p c i e", i=NEXP),
                                        pr[:].unsqueeze(3).broadcast_to([IC, 4, NEXP, NEXP]),
                                        pr[:].unsqueeze(2).broadcast_to([IC, 4, NEXP, NEXP]),
                                        ALU.is_gt).then_inc(bigger_done, 1)

            def top2(dve, body):
                dve.wait_ge(pairs_done, body.at(1, f=1))
                nc.vector.tensor_reduce(s_col[:], pairs[:].rearrange("p c (i e) -> p c e i", i=NEXP), AX.X, ALU.add)
                nc.vector.tensor_reduce(s_row[:], pairs[:].rearrange("p c (i e) -> p c i e", i=NEXP), AX.X, ALU.add)
                dve.drain()
                nc.vector.tensor_tensor(rank[:], s_col[:], s_row[:], ALU.subtract)
                dve.drain()
                nc.vector.tensor_tensor(rank[:], rank[:], e_index[:].rearrange("p (c e) -> p c e", c=4), ALU.add)
                dve.drain()
                nc.vector.scalar_tensor_tensor(out=cw[:], in0=rank[:], scalar=1.5, in1=pr[:],
                                               op0=ALU.is_lt, op1=ALU.mult).then_inc(cw_done, 1)

            def threshold(dve, body, u, newton):
                zu, cd = z[u % 2], cand[u % 2]
                def own(n):
                    dve.wait_ge(z_read, body.at(3 * u + n, h=3 * UNITS))
                wait(dve, over_done, body.at(u - 1, h=UNITS))
                dve.wait_ge(z_done, body.at(u + 1, h=UNITS))
                dve.nop(nofuse=True)
                for c in range(2):
                    nc.vector.max(cd[0:NI[c], c, 0:8], zu[0:NI[c], c * TP:c * TP + T])
                dve.drain()
                for c in range(2):
                    nc.vector.match_replace(z_rest[c][0:NI[c], :], cd[0:NI[c], c, 0:8],
                                            zu[0:NI[c], c * TP:c * TP + T], NEG)
                dve.drain()
                for c in range(2):
                    last = nc.vector.max(cd[0:NI[c], c, 8:16], z_rest[c][0:NI[c], :])
                last.then_inc(z_read, 1)
                own(1)
                nc.vector.tensor_tensor_scan(sums[:], seg[:], cd[:].rearrange("p c r -> p (c r)"), 0.0,
                                             ALU.mult, ALU.add).then_inc(z_read, 1)
                own(2)
                nc.vector.scalar_tensor_tensor(out=taus[:], in0=sums[:], scalar=-1.0, in1=rinv[:],
                                               op0=ALU.add, op1=ALU.mult).then_inc(z_read, 1)
                own(3)
                i = nc.vector.tensor_reduce(ntau[u % 2][:], taus[:].rearrange("p (c r) -> p c r", c=2), AX.X, ALU.max,
                                            negate=True)
                if newton:
                    dve.drain()
                    with dve.Fori(0, NEWTON) as _:
                        for c in range(2):
                            n = NI[c]
                            zc, nt = zu[0:n, c * TP:c * TP + T], ntau[u % 2][0:n, c:c + 1]
                            nc.vector.tensor_scalar(z_rest[c][0:n, :], zc, nt, 0.0, ALU.add, ALU.max)
                            dve.drain()
                            nc.vector.tensor_reduce(nsum[0:n, c:c + 1], z_rest[c][0:n, :], AX.X, ALU.add)
                            dve.drain()
                            nc.vector.tensor_scalar(z_rest[c][0:n, :], z_rest[c][0:n, :], 0.0, None, ALU.is_gt)
                            dve.drain()
                            nc.vector.tensor_reduce(ncnt[0:n, c:c + 1], z_rest[c][0:n, :], AX.X, ALU.add)
                            dve.drain()
                            nc.vector.reciprocal(nrec[0:n, c:c + 1], ncnt[0:n, c:c + 1])
                            dve.drain()
                            nc.vector.scalar_tensor_tensor(out=nsum[0:n, c:c + 1], in0=nsum[0:n, c:c + 1], scalar=-1.0,
                                                           in1=nrec[0:n, c:c + 1], op0=ALU.add, op1=ALU.mult)
                            dve.drain()
                            nc.vector.tensor_tensor(nt, nt, nsum[0:n, c:c + 1], ALU.subtract)
                            dve.drain()
                    i = nc.vector.tensor_copy(nrec[0:1, 0:1], nrec[0:1, 0:1])
                i.then_inc(ntau_done, 1)

            def dve_body(dve, body, newton):
                for s in range(SLOTS + 1):
                    if body.f and s < BLOCKS and not act_rounds(s):
                        dve.wait_ge(gelu_done, body.at(s + 1, f=BLOCKS))
                        nc.vector.tensor_copy(g_hi[s % 4][:], g_raw[s % 2]).then_inc(g_hi_dve, 1)
                    if body.f and s >= 10 and (s - 10) % 4 == 0 and (s - 10) // 4 <= NEXP:
                        c = (s - 10) // 4
                        if c == 0:
                            wait(dve, out_stored, body.at(0, f=1) * 16)
                            dve.wait_ge(dn_done, body.at(1, f=9))
                            nc.vector.scalar_tensor_tensor(out=acc[:], in0=dn[:, 0:NT], scalar=sb2_sum[:], in1=h2[:],
                                                           op0=ALU.add, op1=ALU.add).then_inc(comb_done, 1)
                        else:
                            e = c - 1
                            wait_read(dve, body, use_of(body, "cwB", e))
                            wait(dve, acc_done, body.at(e - 1, f=8))
                            dve.wait_ge(dn_done, body.at(c + 1, f=9))
                            nc.vector.tensor_tensor(tmp[e % 2], dn[:, 0:NT], cwB[e % 2], ALU.mult).then_inc(comb_done, 1)
                    u = scores_at(s)
                    if body.h and u is not None:
                        threshold(dve, body, u, newton)
                    u = transposes_at(s)
                    if body.h and u is not None:
                        dve.wait_ge(at_hi_done, body.at(u + 1, h=UNITS))
                        nc.vector.tensor_tensor(at_lo[u % 2][:, :, 0:T], at[0:IC, 0:NT].rearrange("p (c t) -> p c t", c=2)[:, :, 0:T],
                                                at_hi[u % 2][:, :, 0:T].bitcast(F32), ALU.subtract).then_inc(at_lo_done, 1)
                    if body.h and s == OUT_AT:
                        dve.wait_ge(res_loaded, body.at(1, h=1) * 16)
                        dve.wait_ge(y_done, body.at(1, h=1))
                        nc.vector.scalar_tensor_tensor(out=h2[:], in0=y[:, 0:NT], scalar=bo[:], in1=h_res[:],
                                                       op0=ALU.add, op1=ALU.add).then_inc(h2_done, 1)
                    if body.h and s in LN2:
                        dve.wait_ge(ln2_pe, body.at({"var": 1, "spread": 2}[LN2[s]], h=2))
                        if LN2[s] == "var":
                            nc.vector.tensor_scalar(ve[:], z[0][0:IC, 0:4], EPS, None, ALU.add).then_inc(ln2_ve, 1)
                        else:
                            nc.vector.tensor_tensor(xc[:], xc[:], z[0][:, 0:NT], ALU.mult)
                            dve.drain()
                            nc.vector.tensor_copy(x2_hi[:], xc[:])
                            dve.drain()
                            nc.vector.tensor_tensor(x2_lo[:], xc[:], x2_hi[:].bitcast(F32), ALU.subtract).then_inc(x2_done, 1)
                    if body.f and s == 3:
                        softmax(dve, body)
                    if body.f and s == 5:
                        top2(dve, body)
                    for k, khi, what, arg in uses(body, s):
                        dve_shared(dve, body, k, khi, what, arg)

            def pool_body(pool, body, newton):
                for s in range(SLOTS + 1):
                    if loads_weights(body) and s % 4 == 3 and s // 4 < NE:
                        pool_weights(pool, s // 4)
                    if body.f and s < BLOCKS:
                        pool.wait_ge(*g_hi_ready(body, s))
                        nc.gpsimd.tensor_tensor(g_lo[s % 4][:], g_raw[s % 2], g_hi[s % 4][:].bitcast(F32),
                                                ALU.subtract).then_inc(g_lo_done, 1)
                    if body.f and s == 3:
                        pool.wait_ge(bigger_done, body.at(1, f=1))
                        nc.gpsimd.tensor_tensor(pairs[:], bigger[:], later[:].unsqueeze(1).broadcast_to([IC, 4, NEXP * NEXP]),
                                                ALU.mult).then_inc(pairs_done, 1)
                    u = attention_at(s)
                    if body.h and u is not None:
                        pool.wait_ge(ntau_done, body.at(u + 1, h=UNITS))
                        nc.gpsimd.tensor_tensor(over[:], cand[u % 2][:, :, 15], ntau[u % 2][:], ALU.add).then_inc(over_done, 1)
                        pool.drain()
                        nc.gpsimd.tensor_scalar(over[:], over[:], 0.0, None, ALU.is_gt)
                        pool.drain()
                        nc.gpsimd.tensor_tensor(worst[:], worst[:], over[:], ALU.add)
                        pool.drain()
                    for _, _, what, _ in uses(body, s):
                        if what == "var":
                            pool.wait_ge(ln1_ve, body.at(1, n=1))
                            nc.gpsimd.tensor_tensor(rs[:], ve[:], mhalf[:], ALU.pow).then_inc(ln1_rs, 1)
                    if body.h and LN2.get(s) == "var":
                        pool.wait_ge(ln2_ve, body.at(1, h=1))
                        nc.gpsimd.tensor_tensor(rs[:], ve[:], mhalf[:], ALU.pow).then_inc(ln2_rs, 1)
                    if body.f and s >= 14 and (s - 14) % 4 == 0 and (s - 14) // 4 < NEXP:
                        e = (s - 14) // 4
                        pool.wait_ge(comb_done, body.at(e + 2, f=9))
                        nc.gpsimd.tensor_tensor(acc[:], acc[:], tmp[e % 2], ALU.add).then_inc(acc_done, 1)

            with nc.Block() as block:
                @block.sync
                def _(sp):
                    bodies(sp, lambda b, nw: sp_body(sp, b, nw), 0, False)
                    sp.wait_ge(out_stored, 16 * G)
                    sp.wait_ge(flag_done, 1)
                    rows = sp.value_load(flag[0:1, 0:1])
                    either(sp, rows, lambda: (bodies(sp, lambda b, nw: sp_body(sp, b, nw), 1, True),
                                              sp.wait_ge(out_stored, 32 * G)))

                @block.scalar
                def _(act):
                    act.wait_ge(ready, 1)
                    bodies(act, lambda b, nw: act_body(act, b, nw), 0, False)
                    act.wait_ge(flag_done, 1)
                    rows = act.value_load(flag[0:1, 0:1])
                    either(act, rows, lambda: bodies(act, lambda b, nw: act_body(act, b, nw), 1, True))

                @block.gpsimd
                def _(pool):
                    pool.wait_ge(ready, 1)
                    bodies(pool, lambda b, nw: pool_body(pool, b, nw), 0, False)
                    pool.drain().then_inc(worst_done, 1)
                    pool.wait_ge(flag_done, 1)
                    rows = pool.value_load(flag[0:1, 0:1])
                    either(pool, rows, lambda: bodies(pool, lambda b, nw: pool_body(pool, b, nw), 1, True))

                @block.vector
                def _(dve):
                    nc.vector.memset(at[:], 0.0)
                    for r in range(2):
                        nc.vector.memset(at_hi[r][:, :, T:TP].bitcast(F32), 0.0)
                        nc.vector.memset(at_lo[r][:, :, T:TP].bitcast(F32), 0.0)
                        nc.vector.memset(cand[r][:], 0.0)
                    dve.drain()
                    nc.vector.memset(nrec[:], 1.0).then_inc(ready, 1)
                    bodies(dve, lambda b, nw: dve_body(dve, b, nw), 0, False)
                    dve.wait_ge(worst_done, 1)
                    nc.vector.tensor_scalar(nsum[:], worst[:], 0.0, float(P), ALU.is_gt, ALU.mult)
                    nc.vector.drain().then_inc(flag_sum, 1)
                    dve.wait_ge(flag_sum, 2)
                    nc.vector.tensor_copy(flag[:], shb[0][0:1, 0:1]).then_inc(flag_done, 1)
                    dve.wait_ge(flag_done, 1)
                    rows = dve.value_load(flag[0:1, 0:1])
                    either(dve, rows, lambda: bodies(dve, lambda b, nw: dve_body(dve, b, nw), 1, True))

                @block.tensor
                def _(pe):
                    pe.wait_ge(ready, 1)
                    bodies(pe, lambda b, nw: pe_body(pe, b, nw), 0, False)
                    pe.wait_ge(flag_sum, 1)
                    for c in range(2):
                        last = nc.tensor.matmul(shb[0][0:1, 0:1], nsum[0:NI[c], c:c + 1], mean_w[0:NI[c], 0:1],
                                                start=c == 0, stop=c == 1)
                    last.then_inc(flag_sum, 1)
                    pe.wait_ge(flag_done, 1)
                    rows = pe.value_load(flag[0:1, 0:1])
                    either(pe, rows, lambda: bodies(pe, lambda b, nw: pe_body(pe, b, nw), 1, True))


def kernel(x, L0_tok_W0, L0_tok_b0, L0_tok_pos0, L0_tok_W1, L0_tok_b1, L0_tok_pos1, L0_tok_W2, L0_tok_b2,
           L0_tok_pos2, L0_tok_scale_emb, L0_attn_W_qkv, L0_attn_W_out, L0_attn_b_out, L0_ffn_gate_w,
           L0_ffn_gate_b, L0_ffn_sw1, L0_ffn_sb1, L0_ffn_sw2, L0_ffn_sb2, L0_ffn_rw1, L0_ffn_rb1,
           L0_ffn_rw2, L0_ffn_rb2):
    import numpy as np
    import concourse.bacc as bacc
    from concourse.bass_utils import run_bass_kernel_spmd

    def arr(v):
        return np.asarray(v)

    xt = arr(x).reshape(G, NB, CTX // 4, 4, P).transpose(0, 4, 1, 3, 2)
    xT = np.zeros((G, P, NB, XR, XM), xt.dtype)
    xT[..., :CTX // 4] = xt

    def patch_weights(w, p):
        return arr(w).reshape(P, p, P).transpose(2, 1, 0).reshape(P, p * P)

    def column(v):
        return arr(v).reshape(-1, 1)

    wqkv = arr(L0_attn_W_qkv)
    inner = HEADS * DH
    w1 = np.concatenate([arr(L0_ffn_sw1), arr(L0_ffn_rw1)])
    w2 = np.concatenate([arr(L0_ffn_sw2), arr(L0_ffn_rw2)])
    up_w = w1.transpose(0, 2, 1)
    dn_w = w2.reshape(-1, P, FB, P).transpose(0, 3, 2, 1).reshape(-1, P, FF)
    ins = {
        "xT": xT.reshape(G, P, NB * XB),
        "w0T": patch_weights(L0_tok_W0, PATCH[0]),
        "w1T": patch_weights(L0_tok_W1, PATCH[1]),
        "w2T": patch_weights(L0_tok_W2, PATCH[2]),
        "posT": np.concatenate([arr(v)[0] for v in (L0_tok_pos0, L0_tok_pos1, L0_tok_pos2)]).T,
        "b0": column(L0_tok_b0), "b1": column(L0_tok_b1), "b2": column(L0_tok_b2),
        "seT": arr(L0_tok_scale_emb).T,
        "wqkT": wqkv[:, :2 * inner],
        "wvT": wqkv[:, 2 * inner:].reshape(P, HEADS, DH).transpose(2, 1, 0).reshape(DH, HEADS * P),
        "woutT": arr(L0_attn_W_out).reshape(HEADS, DH, P).transpose(1, 0, 2).reshape(DH, HEADS * P),
        "b_out": column(L0_attn_b_out),
        "gateT": arr(L0_ffn_gate_w).T,
        "gate_b": arr(L0_ffn_gate_b),
        "ew": np.concatenate([up_w, dn_w], axis=2),
        "eb1": np.concatenate([arr(L0_ffn_sb1), arr(L0_ffn_rb1)]).reshape(BLOCKS, P).T,
        "sb2T": arr(L0_ffn_sb2).T,
        "rb2": arr(L0_ffn_rb2),
    }
    nc = bacc.Bacc("TRN2", target_bir_lowering=False, num_devices=1)
    arrays, args = {}, []
    for name, v in ins.items():
        v = np.ascontiguousarray(v)
        arrays[f"in_{name}"] = v
        args.append(nc.dram_tensor(f"in_{name}", v.shape, mybir.dt.from_np(v.dtype), kind="ExternalInput").ap())
    out = nc.dram_tensor("out_T", (G, P, NT), F32, kind="ExternalOutput").ap()
    build(nc, *args, out)
    r = run_bass_kernel_spmd(nc, [arrays], core_ids=[0])
    got = r.results[0]["out_T"].reshape(G, P, NB, TP)[..., :T]
    return np.ascontiguousarray(got.transpose(0, 2, 3, 1).reshape(BATCH, T, P))
```

```python
from contextlib import ExitStack

import concourse.bass as bass
from concourse import mybir

F32 = mybir.dt.float32
F32R = mybir.dt.float32r
I32 = mybir.dt.int32
ACT = mybir.ActivationFunctionType
ALU = mybir.AluOpType
AX = mybir.AxisListType

P = 128
PATCH = (8, 16, 32)
CTX = 512
NTOK = tuple((CTX - p) // (p // 2) + 1 for p in PATCH)
TOFF = (0, NTOK[0], NTOK[0] + NTOK[1])
T = sum(NTOK)
TP = T + 1
NB = 2
NT = NB * TP
IC = TP // 2
NI = (IC, T - IC)
BATCH = 64
G = BATCH // NB
HEADS, DH = 8, 64
HALF = HEADS // 2 * P
NEXP, NSH = 8, 2
FF = 512
FB = FF // P
BLOCKS = (NSH + NEXP) * FB
EPS = 1e-5
NEG = -3.0e38

XR, XM = 4, CTX // 4 + 4
XB = XR * XM
SB = 8
STEPS = BATCH // SB
CW = 2 * XB
WCH = 1024

LAG = 3
SLOTS = BLOCKS + LAG
UNITS = NB * HEADS
NEWTON = 24


def head_of(u):
    return u // 4, (u // 2) % 2, u % 2


def unit_at(s, first):
    return (s - first) // 2 if (s - first) % 2 == 0 and 0 <= (s - first) // 2 < UNITS else None


def scores_at(s):
    return unit_at(s, -1) if s > 3 else {0: 1, 2: 2}.get(s)


SCORES0_AT, ATTENTION0_AT = 38, 40


def attention_at(s):
    return unit_at(s, 1)


def transposes_at(s):
    return unit_at(s, 2)


def values_at(s):
    return unit_at(s, 4) if s > 5 else 0 if s == 5 else None


ACT_ROUNDS = (1, 3)
OUT_AT = 35
SHARED = {1: [("logits", 0, "f")], 7: [("cwT", 0, "f")],
          5: [("q", 2, "h")], 6: [("k", 2, "h")], 14: [("q", 3, "h")], 16: [("k", 3, "h")],
          10: [("mean", 0, "n")], 12: [("var", 0, "n")], 18: [("spread", 0, "n")],
          20: [("v", (0, 0, 0), "n")], 22: [("q", 0, "n")], 24: [("v", (0, 1, 0), "n")],
          25: [("k", 0, "n")], 26: [("v", (1, 0, 0), "n")], 28: [("v", (1, 1, 0), "n")],
          30: [("q", 1, "n")], 32: [("k", 1, "n")],
          34: [("v", (0, 0, 1), "n")], 36: [("mean2", 0, "h")], 37: [("v", (0, 1, 1), "n")],
          40: [("v", (1, 0, 1), "n")], 42: [("v", (1, 1, 1), "n")]}
for _e in range(NEXP):
    SHARED.setdefault(9 + 4 * _e if _e else 11, []).append(("cwB", _e, "f"))
EXP_AT, SOFTMAX_AT, TOP2_AT = 4, 4, 5
SQUARE1_AT, SQUARE2_AT = 11, 37
LN2 = {38: "var", 40: "spread"}
N_SHARED = {k: sum(x[2] == k for v in SHARED.values() for x in v) for k in "fhn"}


class Body:

    def __init__(self, f, h, n, nf, nh, nn, g, i=None):
        self.f, self.h, self.n = f, h, n
        self.nf, self.nh, self.nn = nf, nh, nn
        self.g, self.i = g, i

    def at(self, count, f=0, h=0, n=0):
        static = self.nf * f + self.nh * h + self.nn * n + count
        if self.i is None:
            return static
        return self.i * (f * self.f + h * self.h + n * self.n) + static


def wait(eng, sem, value):
    if not isinstance(value, int) or value > 0:
        eng.wait_ge(sem, value)


def build(nc, xT, w0T, w1T, w2T, posT, b0, b1, b2, seT, wqkT, wvT, woutT, b_out,
          gateT, gate_b, ew, eb1, sb2T, rb2, out):
    hs = nc.dram_tensor("h_scratch", (G, P, NT), F32, kind="Internal").ap()

    with ExitStack() as keep:
        def sbuf(name, shape, dt=F32, ctx=keep):
            return ctx.enter_context(nc.sbuf_tensor(name, shape, dt))

        def sem(name):
            return keep.enter_context(nc.semaphore(name))

        banks = [keep.enter_context(nc.psum_tensor(f"bank{i}", [P, 512], F32)) for i in range(8)]

        wqk_hi, wqk_lo = sbuf("wqk_hi", [P, 1024], F32R), sbuf("wqk_lo", [P, 1024], F32R)
        wvo_hi, wvo_lo = sbuf("wvo_hi", [P, 1024], F32R), sbuf("wvo_lo", [P, 1024], F32R)
        gate_hi, gate_lo = sbuf("gate_hi", [P, NEXP], F32R), sbuf("gate_lo", [P, NEXP], F32R)
        gate_raw = sbuf("gate_raw", [P, NEXP])
        rb2_raw = sbuf("rb2_raw", [NEXP, P])
        rb2_hi, rb2_lo = sbuf("rb2_hi", [NEXP, P], F32R), sbuf("rb2_lo", [NEXP, P], F32R)
        gb = sbuf("gb", [P, NEXP])
        bo = sbuf("bo", [P, 1])
        up_bias = sbuf("up_bias", [P, BLOCKS])
        sb2 = sbuf("sb2", [P, NSH])
        sb2_sum = sbuf("sb2_sum", [P, 1])
        ident = sbuf("ident", [P, P])
        id8 = sbuf("id8", [NEXP, NEXP], F32R)
        mean_w = sbuf("mean_w", [P, P])
        later = sbuf("later", [IC, NEXP * NEXP])
        e_index = sbuf("e_index", [IC, 4 * NEXP])
        rinv = sbuf("rinv", [IC, 32])
        seg = sbuf("seg", [IC, 32])
        mhalf = sbuf("mhalf", [IC, 4])
        worst = sbuf("worst", [IC, 2])
        flag = sbuf("flag", [1, 1], I32)

        with ExitStack() as first:
            def sb1(name, shape, dt=F32):
                return sbuf(name, shape, dt, first)

            wcols = (PATCH[0] * P, PATCH[1] * P, PATCH[2] * P)
            w_hi = [sb1(f"w{i}_hi", [P, n], F32R) for i, n in enumerate(wcols)]
            w_lo = [sb1(f"w{i}_lo", [P, n], F32R) for i, n in enumerate(wcols)]
            x_hi = [sb1(f"x_hi{i}", [P, SB * XB], F32R) for i in range(2)]
            x_lo = [sb1(f"x_lo{i}", [P, SB * XB], F32R) for i in range(2)]
            raw = [sb1(f"raw{i}", [P, CW]) for i in range(2)]
            stage = [sb1(f"stage{i}", [P, SB, TP]) for i in range(2)]
            table = sb1("table", [P, T])
            bvec, svec = sb1("bvec", [P, 3]), sb1("svec", [P, 3])
            wv_raw, wo_raw = sb1("wv_raw", [DH, 1024]), sb1("wo_raw", [DH, 1024])

            small = sem("small_loaded")
            memset_done = sem("memset_done")
            raw_loaded = [sem("raw_loaded0"), sem("raw_loaded1")]
            hi_done = sem("hi_done")
            lo_done = sem("lo_done")
            const_done = sem("const_done")
            fold_done = sem("fold_done")
            fold_hi = sem("fold_hi")
            fold_lo = sem("fold_lo")
            emb_done = sem("emb_done")
            emb_out = sem("emb_out")
            h_stored = [sem("h_stored0"), sem("h_stored1")]

            chunks = [("w", 0, 0)] + [("x", 0, q) for q in range(4)] + [("w", 1, 0), ("w", 1, 1)]
            chunks += [("w", 2, q) for q in range(4)] + [("qk", 0, 0)]
            FIRSTC = len(chunks)

            def chunk_no(k, q):
                return q + 1 if isinstance(k, int) and k == 0 else (k - 1) * 4 + FIRSTC + q

            def loaded_value(c, par):
                return (c - par) * 8 + 16

            with nc.Block() as block:
                @block.sync
                def _(sp):
                    sp.dma_start(wv_raw[:], wvT).then_inc(small, 16)
                    sp.dma_start(wo_raw[:], woutT).then_inc(small, 16)
                    for c, (kind, a, q) in enumerate(chunks):
                        wait(sp, lo_done, c - 1)
                        src = {"w": (w0T, w1T, w2T)[a][:, q * WCH:(q + 1) * WCH] if kind == "w" else None,
                               "x": xT[q], "qk": wqkT}[kind]
                        n = CW if kind == "x" else WCH
                        sp.dma_start(raw[c % 2][:, 0:n], src).then_inc(raw_loaded[c % 2], 16)

                    def step(k, par):
                        for q in range(4):
                            c = chunk_no(k + 1, q)
                            sp.wait_ge(lo_done, c - 1)
                            sp.dma_start(raw[q % 2][:, :], xT[(k + 1) * 4 + q]).then_inc(raw_loaded[q % 2], 16)
                        store(k, par)

                    def store(k, par):
                        sp.wait_ge(emb_out, k * 4 + 4)
                        sp.dma_start(hs[bass.ds(k * 4, 4)].rearrange("g p (b t) -> p g b t", b=NB),
                                     stage[par][:].rearrange("p (g b) t -> p g b t", b=NB)).then_inc(h_stored[par], 16)

                    step(0, 0)
                    with sp.Fori(0, (STEPS - 2) // 2) as i:
                        step(i * 2 + 1, 1)
                        step(i * 2 + 2, 0)
                    store(STEPS - 1, 1)
                    for par in range(2):
                        sp.wait_ge(h_stored[par], 16 * STEPS // 2)

                @block.gpsimd
                def _(pool):
                    nc.gpsimd.memset(ident[:], 0.0)
                    nc.gpsimd.memset(later[:], 0.0)
                    nc.gpsimd.memset(mean_w[:], 1.0 / P)
                    nc.gpsimd.memset(seg[:], 1.0)
                    nc.gpsimd.memset(mhalf[:], -0.5)
                    nc.gpsimd.memset(worst[:], 0.0)
                    for r in range(16):
                        nc.gpsimd.memset(rinv[:, r:r + 17:16], 1.0 / (r + 1))
                    for e in range(NEXP):
                        nc.gpsimd.memset(e_index[:, e:e + 3 * NEXP + 1:NEXP], float(e))
                    for par in range(2):
                        nc.gpsimd.memset(stage[par][:, :, T:TP], 0.0)
                    pool.drain()
                    nc.gpsimd.memset(seg[:, 0:17:16], 0.0)
                    for first_e in range(1, NEXP):
                        nc.gpsimd.memset(later[:, first_e * NEXP:first_e * NEXP + first_e], 1.0)
                    nc.gpsimd.affine_select(out=ident[:], in_=ident[:], compare_op=ALU.not_equal, fill=1.0,
                                            base=0, pattern=[[-1, P]], channel_multiplier=1)
                    pool.drain()
                    nc.gpsimd.memset(flag[:], 0).then_inc(memset_done, 1)

                @block.scalar
                def _(act):
                    for dst, src in ((gate_raw, gateT), (rb2_raw, rb2), (bo, b_out), (up_bias, eb1),
                                     (sb2, sb2T), (table, posT), (svec, seT)):
                        act.dma_start(dst[:], src).then_inc(small, 16)
                    for s, b in enumerate((b0, b1, b2)):
                        act.dma_start(bvec[:, s:s + 1], b).then_inc(small, 16)
                    act.dma_start(gb[:], gate_b.partition_broadcast(P)).then_inc(small, 16)
                    for half in range(2):
                        act.wait_ge(fold_done, half + 1)
                        nc.scalar.activation(wvo_hi[:, half * HALF:(half + 1) * HALF], banks[half][:],
                                             ACT.Copy).then_inc(fold_hi, 1)
                    for c, (kind, a, q) in enumerate(chunks):
                        act.wait_ge(raw_loaded[c % 2], loaded_value(c, c % 2))
                        dst = (x_hi[0][:, q * CW:(q + 1) * CW] if kind == "x" else wqk_hi[:] if kind == "qk"
                               else w_hi[a][:, q * WCH:(q + 1) * WCH])
                        n = CW if kind == "x" else WCH
                        nc.scalar.activation(dst, raw[c % 2][:, 0:n], ACT.Copy).then_inc(hi_done, 1)

                    def step(k, par):
                        if not isinstance(k, int) or k >= 2:
                            act.wait_ge(emb_done, k * 4 - 4)
                        for q in range(4):
                            c = chunk_no(k, q)
                            act.wait_ge(raw_loaded[q % 2], loaded_value(c, q % 2))
                            nc.scalar.activation(x_hi[par][:, q * CW:(q + 1) * CW], raw[q % 2][:],
                                                 ACT.Copy).then_inc(hi_done, 1)

                    step(1, 1)
                    with act.Fori(0, (STEPS - 2) // 2) as i:
                        step(i * 2 + 2, 0)
                        step(i * 2 + 3, 1)

                @block.vector
                def _(dve):
                    for half in range(2):
                        cols = slice(half * HALF, (half + 1) * HALF)
                        dve.wait_ge(fold_hi, half + 1)
                        nc.vector.tensor_tensor(wvo_lo[:, cols], banks[half][:], wvo_hi[:, cols].bitcast(F32),
                                                ALU.subtract).then_inc(fold_lo, 1)
                    dve.wait_ge(small, 13 * 16)
                    dve.wait_ge(memset_done, 1)
                    nc.vector.tensor_copy(gate_hi[:], gate_raw[:])
                    nc.vector.tensor_copy(rb2_hi[:], rb2_raw[:])
                    nc.vector.tensor_copy(id8[:], ident[0:NEXP, 0:NEXP])
                    nc.vector.tensor_tensor(bvec[:], bvec[:], svec[:], ALU.add)
                    nc.vector.tensor_tensor(sb2_sum[:], sb2[:, 0:1], sb2[:, 1:2], ALU.add)
                    dve.drain()
                    nc.vector.tensor_tensor(gate_lo[:], gate_raw[:], gate_hi[:].bitcast(F32), ALU.subtract)
                    nc.vector.tensor_tensor(rb2_lo[:], rb2_raw[:], rb2_hi[:].bitcast(F32), ALU.subtract)
                    for s in range(3):
                        cols = slice(TOFF[s], TOFF[s] + NTOK[s])
                        nc.vector.tensor_scalar(table[:, cols], table[:, cols], bvec[:, s:s + 1], None, ALU.add)
                    dve.drain()
                    for c, (kind, a, q) in enumerate(chunks):
                        dst, hi = ((x_lo[0][:, q * CW:(q + 1) * CW], x_hi[0][:, q * CW:(q + 1) * CW]) if kind == "x" else
                                   (wqk_lo[:], wqk_hi[:]) if kind == "qk" else
                                   (w_lo[a][:, q * WCH:(q + 1) * WCH], w_hi[a][:, q * WCH:(q + 1) * WCH]))
                        n = CW if kind == "x" else WCH
                        dve.wait_ge(hi_done, c + 1)
                        nc.vector.tensor_tensor(dst, raw[c % 2][:, 0:n], hi.bitcast(F32),
                                                ALU.subtract).then_inc(lo_done, 1)

                    def low(k, par):
                        for q in range(4):
                            dve.wait_ge(hi_done, chunk_no(k, q) + 1)
                            cols = slice(q * CW, (q + 1) * CW)
                            nc.vector.tensor_tensor(x_lo[par][:, cols], raw[q % 2][:], x_hi[par][:, cols].bitcast(F32),
                                                    ALU.subtract).then_inc(lo_done, 1)

                    def bank_out(k, par, use, dst_b, nb, s, width):
                        n, off = NTOK[s], TOFF[s]
                        dve.wait_ge(emb_done, k * 4 + use + 1)
                        src = banks[par * 4 + use][:, 0:nb * width].rearrange("p (b t) -> p b t", b=nb)[:, :, 0:n]
                        add = table[:, off:off + n].unsqueeze(1).broadcast_to([P, nb, n])
                        nc.vector.tensor_tensor(stage[par][:, dst_b:dst_b + nb, off:off + n], src, add,
                                                ALU.add).then_inc(emb_out, 1)

                    def outs(k, par, wait_store):
                        if wait_store is not None:
                            dve.wait_ge(h_stored[par], wait_store)
                        bank_out(k, par, 0, 0, 4, 0, NTOK[0] + 1)
                        bank_out(k, par, 1, 4, 4, 0, NTOK[0] + 1)
                        bank_out(k, par, 2, 0, SB, 1, NTOK[1] + 1)
                        bank_out(k, par, 3, 0, SB, 2, NTOK[2] + 1)

                    low(1, 1)
                    outs(0, 0, None)
                    low(2, 0)
                    outs(1, 1, None)
                    with dve.Fori(0, (STEPS - 4) // 2) as i:
                        low(i * 2 + 3, 1)
                        outs(i * 2 + 2, 0, i * 16 + 16)
                        low(i * 2 + 4, 0)
                        outs(i * 2 + 3, 1, i * 16 + 16)
                    low(STEPS - 1, 1)
                    outs(STEPS - 2, 0, (STEPS // 2 - 1) * 16)
                    outs(STEPS - 1, 1, (STEPS // 2 - 1) * 16)

                @block.tensor
                def _(pe):
                    pe.wait_ge(small, 13 * 16)
                    for half in range(2):
                        for j in range(HEADS // 2):
                            h = half * HEADS // 2 + j
                            last = nc.tensor.matmul(banks[half][:, j * P:(j + 1) * P], wv_raw[:, h * P:(h + 1) * P],
                                                    wo_raw[:, h * P:(h + 1) * P], start=True, stop=True)
                        last.then_inc(fold_done, 1)

                    def products(out_ap, s, j, par, b0_, nb, n, first_, last_):
                        st = PATCH[s] // 8
                        def moving(x):
                            v = x[par][:].rearrange("p (b r m) -> p b r m", b=SB, r=XR)
                            return v[:, b0_:b0_ + nb, j % XR, j // XR:j // XR + st * (n - 1) + 1:st]
                        cols = slice(j * P, (j + 1) * P)
                        nc.tensor.matmul(out_ap, w_hi[s][:, cols], moving(x_hi), start=first_, stop=False)
                        nc.tensor.matmul(out_ap, w_hi[s][:, cols], moving(x_lo), start=False, stop=False)
                        return nc.tensor.matmul(out_ap, w_lo[s][:, cols], moving(x_hi), start=False, stop=last_)

                    def step(k, par, cold=False):
                        if not isinstance(k, int) or k >= 2:
                            pe.wait_ge(emb_out, k * 4 - 4)
                        if cold:
                            pe.wait_ge(fold_lo, 2)
                        for use, s, b0_, nb in ((0, 0, 0, 4), (1, 0, 4, 4), (2, 1, 0, SB), (3, 2, 0, SB)):
                            n = NTOK[s] + 1
                            if use < 2:
                                pe.wait_ge(lo_done, chunk_no(k, 2 * use + 1) + 1)
                            elif cold:
                                pe.wait_ge(lo_done, 7 if s == 1 else 11)
                            o = banks[par * 4 + use][:, 0:nb * n]
                            for j in range(PATCH[s]):
                                last = products(o, s, j, par, b0_, nb, n, j == 0, j == PATCH[s] - 1)
                            last.then_inc(emb_done, 1)

                    step(0, 0, True)
                    step(1, 1)
                    with pe.Fori(0, (STEPS - 2) // 2) as i:
                        step(i * 2 + 2, 0)
                        step(i * 2 + 3, 1)

        with ExitStack() as second:
            def sb(name, shape, dt=F32):
                return sbuf(name, shape, dt, second)

            NE = (NSH + NEXP)
            ew_hi, ew_lo = sb("ew_hi", [P, NE * WCH], F32R), sb("ew_lo", [P, NE * WCH], F32R)
            rings = sb("rings", [P, 6 * NT])
            cwB = [rings[:, i * NT:(i + 1) * NT] for i in range(2)]
            g_raw = [rings[:, (2 + i) * NT:(3 + i) * NT] for i in range(2)]
            tmp = [rings[:, (4 + i) * NT:(5 + i) * NT] for i in range(2)]
            wst = [rings[:, i * WCH:(i + 1) * WCH] for i in range(2)]
            x1_hi, x1_lo = sb("x1_hi", [P, NT], F32R), sb("x1_lo", [P, NT], F32R)
            x2_hi, x2_lo = sb("x2_hi", [P, NT], F32R), sb("x2_lo", [P, NT], F32R)
            qk_hi = {(w, r): sb(f"{w}_hi{r}", [P, NT], F32R) for w in "qk" for r in range(2)}
            qk_lo = {(w, r): sb(f"{w}_lo{r}", [P, NT], F32R) for w in "qk" for r in range(2)}
            v_hi = sb("v_hi", [IC, NB, 2, 2 * HALF], F32R)
            v_lo = sb("v_lo", [IC, NB, 2, 2 * HALF], F32R)
            a = [sb(f"a{r}", [IC, 2, TP]) for r in range(2)]
            at_hi = [sb(f"at_hi{r}", [IC, 2, TP], F32R) for r in range(2)]
            at_lo = [sb(f"at_lo{r}", [IC, 2, TP], F32R) for r in range(2)]
            g_hi = [sb(f"g_hi{r}", [P, NT], F32R) for r in range(4)]
            g_lo = [sb(f"g_lo{r}", [P, NT], F32R) for r in range(4)]
            h_next, h_res, h2, acc = (sb(n, [P, NT]) for n in ("h_next", "h_res", "h2", "acc"))
            xc, sq = sb("xc", [P, NT]), sb("sq", [P, NT])
            cwT_hi, cwT_lo = sb("cwT_hi", [NEXP, NT], F32R), sb("cwT_lo", [NEXP, NT], F32R)
            z_rest = [sb(f"z_rest{i}", [IC, T]) for i in range(2)]
            cand = [sb(f"cand{r}", [IC, 2, 16]) for r in range(2)]
            sums, taus = sb("sums", [IC, 32]), sb("taus", [IC, 32])
            ntau = [sb(f"ntau{r}", [IC, 2]) for r in range(2)]
            over = sb("over", [IC, 2])
            ve, rs = sb("ve", [IC, 4]), sb("rs", [IC, 4])
            lg, ex, pr, cw = (sb(n, [IC, 4, NEXP]) for n in ("lg", "ex", "pr", "cw"))
            lmax, lsum, lrec = (sb(n, [IC, 4]) for n in ("lmax", "lsum", "lrec"))
            bigger = sb("bigger", [IC, 4, NEXP * NEXP])
            pairs = sb("pairs", [IC, 4, NEXP * NEXP])
            s_col, s_row, rank = (sb(n, [IC, 4, NEXP]) for n in ("s_col", "s_row", "rank"))
            nsum, ncnt, nrec = (sb(n, [IC, 2]) for n in ("nsum", "ncnt", "nrec"))

            z = banks[0:2]
            at = banks[2]
            y = banks[3]
            shb = banks[4:6]
            up = banks[6]
            dn = banks[7]

            ready = sem("ready")
            w_loaded = [sem(f"w_loaded{i}") for i in range(2)]
            w_hi_done = sem("w_hi_done")
            w_lo_done = sem("w_lo_done")
            next_loaded = sem("next_loaded")
            res_loaded = sem("res_loaded")
            out_stored = sem("out_stored")
            sh_done = sem("sh_done")
            sh_hi = sem("sh_hi")
            sh_free = [sem("sh_free0"), sem("sh_free1")]
            ln1_xc, ln2_xc = sem("ln1_xc"), sem("ln2_xc")
            ln1_sq, ln2_sq = sem("ln1_sq"), sem("ln2_sq")
            ln1_ve, ln2_ve = sem("ln1_ve"), sem("ln2_ve")
            ln1_rs, ln2_rs = sem("ln1_rs"), sem("ln2_rs")
            x2_done = sem("x2_done")
            ln2_pe = sem("ln2_pe")
            z_done = sem("z_done")
            z_read = sem("z_read")
            ntau_done = sem("ntau_done")
            over_done = sem("over_done")
            relu_done = sem("relu_done")
            at_done = sem("at_done")
            at_hi_done = sem("at_hi_done")
            at_lo_done = sem("at_lo_done")
            y_done = sem("y_done")
            h2_done = sem("h2_done")
            up_done = sem("up_done")
            gelu_done = sem("gelu_done")
            g_hi_act, g_hi_dve = sem("g_hi_act"), sem("g_hi_dve")
            g_lo_done = sem("g_lo_done")
            dn_done = sem("dn_done")
            comb_done = sem("comb_done")
            acc_done = sem("acc_done")
            lg_done = sem("lg_done")
            ex_done = sem("ex_done")
            bigger_done = sem("bigger_done")
            pairs_done = sem("pairs_done")
            cw_done = sem("cw_done")
            flag_sum = sem("flag_sum")
            flag_done = sem("flag_done")
            worst_done = sem("worst_done")

            HAS_HI = ("q", "k", "v", "cwT")

            N_HI = {p: sum(x[2] == p and x[0] in HAS_HI for v in SHARED.values() for x in v) for p in "fhn"}

            def sh_at(body, n):
                return body.at(n, f=N_SHARED["f"], h=N_SHARED["h"], n=N_SHARED["n"])

            def sh_bank(body, k):
                assert body.i is None or sum(N_SHARED.values()) % 2 == 0
                return (body.nf * N_SHARED["f"] + body.nh * N_SHARED["h"] + body.nn * N_SHARED["n"] + k) % 2

            def sh_turn(body, k):
                static = body.nf * N_SHARED["f"] + body.nh * N_SHARED["h"] + body.nn * N_SHARED["n"] + k
                return static // 2 if body.i is None else body.i * (sum(N_SHARED.values()) // 2) + static // 2

            def wait_read(eng, body, k):
                eng.wait_ge(sh_free[sh_bank(body, k)], sh_turn(body, k) + 1)

            def sh_hi_at(body, n):
                return body.at(n, f=N_HI["f"], h=N_HI["h"], n=N_HI["n"])

            def uses(body, s):
                k = khi = 0
                found = []
                for t in sorted(SHARED):
                    for what, arg, part in SHARED[t]:
                        if {"f": body.f, "h": body.h, "n": body.n}[part]:
                            if t == s:
                                found.append((k, khi, what, arg))
                            k += 1
                            khi += what in HAS_HI
                return found

            def use_of(body, what, arg):
                return next(k for t in SHARED for k, _, w, a_ in uses(body, t) if (w, a_) == (what, arg))

            def bodies(eng, emit, base, newton):
                nb = base * G
                emit(Body(0, 0, 1, nb, nb, nb, -1), newton)
                emit(Body(0, 1, 1, nb, nb, nb + 1, 0), newton)
                emit(Body(1, 1, 1, nb, nb + 1, nb + 2, 1), newton)
                with eng.Fori(0, G - 3) as i:
                    emit(Body(1, 1, 1, nb + 1, nb + 2, nb + 3, i + 2, i), newton)
                emit(Body(1, 1, 0, nb + G - 2, nb + G - 1, nb + G, G - 1), newton)
                emit(Body(1, 0, 0, nb + G - 1, nb + G, nb + G, G), newton)

            def this_group(body):
                return lambda count, each: body.at(count, h=each)

            def next_group(body):
                return lambda count, each: body.at(count, n=each)

            def act_rounds(s):
                return s % 4 in ACT_ROUNDS

            def g_hi_ready(body, s):
                before = sum(act_rounds(t) == act_rounds(s) for t in range(s + 1))
                total = sum(act_rounds(t) == act_rounds(s) for t in range(BLOCKS))
                return (g_hi_act if act_rounds(s) else g_hi_dve), body.at(before, f=total)

            def loads_weights(body):
                return isinstance(body.nh, int) and body.nh == 0 and body.h

            def either(eng, flag_reg, general):
                with eng.If(flag_reg > 0):
                    general()
                with eng.Else():
                    eng.nop()

            def sp_body(sp, body):
                if body.n:
                    wait(sp, ln1_xc, body.at(0, n=1))
                    sp.dma_start(h_next[:], hs[body.g + 1]).then_inc(next_loaded, 16)
                if body.h:
                    wait(sp, h2_done, body.at(0, h=1))
                    sp.dma_start(h_res[:], hs[body.g]).then_inc(res_loaded, 16)
                if loads_weights(body):
                    for e in range(NE):
                        wait(sp, w_lo_done, e - 1)
                        sp.dma_start(wst[e % 2], ew[e]).then_inc(w_loaded[e % 2], 16)
                if body.f:
                    sp.wait_ge(acc_done, body.at(8, f=8))
                    sp.dma_start(out[body.g - 1], acc[:]).then_inc(out_stored, 16)

            def three(out_ap, s_hi, s_lo, m_hi, m_lo, start=True, stop=True, share=False):
                kw = {"skip_group_check": True} if share else {}
                nc.tensor.matmul(out_ap, s_hi, m_hi, start=start, stop=False, **kw)
                nc.tensor.matmul(out_ap, s_hi, m_lo, start=False, stop=False, **kw)
                return nc.tensor.matmul(out_ap, s_lo, m_hi, start=False, stop=stop, **kw)

            def ln_product(pe, bank, what, src):
                if what == "mean":
                    return nc.tensor.matmul(bank[:, 0:NT], mean_w[:], src[:], start=True, stop=True)
                for c in range(4):
                    cols = slice(c * IC, (c + 1) * IC)
                    if what == "var":
                        last = nc.tensor.matmul(bank[0:IC, c:c + 1], sq[:, cols], mean_w[:, 0:1],
                                                start=True, stop=True)
                    else:
                        last = nc.tensor.matmul(bank[:, cols], rs[:, c:c + 1].broadcast_to([IC, P]),
                                                ident[0:IC, 0:IC], start=True, stop=True)
                return last

            def pe_shared(pe, body, k, what, arg):
                sh = shb[sh_bank(body, k)]
                wait(pe, sh_free[sh_bank(body, k)], sh_turn(body, k))
                source = None
                if what == "cwB":
                    source = use_of(body, "cwT", 0)
                elif what in ("q", "k", "v") and body.n and k > use_of(body, "spread", 0):
                    source = use_of(body, "spread", 0)
                if source is not None and sh_bank(body, source) != sh_bank(body, k):
                    wait_read(pe, body, source)
                if what == "logits":
                    pe.wait_ge(x2_done, body.at(1, f=1))
                    for c in range(4):
                        cols = slice(c * IC, (c + 1) * IC)
                        last = three(sh[0:IC, c * NEXP:(c + 1) * NEXP], x2_hi[:, cols], x2_lo[:, cols],
                                     gate_hi[:], gate_lo[:])
                elif what == "cwT":
                    pe.wait_ge(cw_done, body.at(1, f=1))
                    for c in range(4):
                        last = nc.tensor.transpose(sh[0:NEXP, c * IC:(c + 1) * IC], cw[:, c, :], ident[0:IC, 0:IC])
                elif what == "cwB":
                    sel = id8[:, arg:arg + 1].broadcast_to([NEXP, P])
                    nc.tensor.matmul(sh[:, 0:NT], sel, cwT_hi[:], start=True, stop=False)
                    last = nc.tensor.matmul(sh[:, 0:NT], sel, cwT_lo[:], start=False, stop=True)
                elif what in "qk":
                    cols = slice((what == "k") * 512 + arg * P, (what == "k") * 512 + (arg + 1) * P)
                    last = three(sh[:, 0:NT], wqk_hi[:, cols], wqk_lo[:, cols], x1_hi[:], x1_lo[:])
                elif what == "v":
                    b, c, half = arg
                    rows = slice(b * TP + c * IC, b * TP + (c + 1) * IC)
                    cols = slice(half * HALF, (half + 1) * HALF)
                    last = three(sh[0:IC, :], x1_hi[:, rows], x1_lo[:, rows], wvo_hi[:, cols], wvo_lo[:, cols])
                elif what == "mean2":
                    pe.wait_ge(h2_done, body.at(1, h=1))
                    last = ln_product(pe, sh, "mean", h2)
                else:
                    if what == "mean":
                        pe.wait_ge(next_loaded, body.at(1, n=1) * 16)
                    elif what == "var":
                        pe.wait_ge(ln1_sq, body.at(1, n=1))
                    else:
                        pe.wait_ge(ln1_rs, body.at(1, n=1))
                    last = ln_product(pe, sh, what, h_next)
                last.then_inc(sh_done, 1)

            def pe_scores(pe, body, u, count):
                p, b, j = head_of(u)
                r, rows = p % 2, slice(j * DH, (j + 1) * DH)
                wait(pe, relu_done, count(u - 1, UNITS))
                if p >= 2:
                    kq, kk = use_of(body, "q", p), use_of(body, "k", p)
                    wait_read(pe, body, kk)
                    if sh_bank(body, kq) != sh_bank(body, kk):
                        wait_read(pe, body, kq)
                for c in range(2):
                    q0 = b * TP + c * IC
                    last = three(z[u % 2][0:NI[c], c * TP:(c + 1) * TP],
                                 qk_hi["q", r][rows, q0:q0 + NI[c]], qk_lo["q", r][rows, q0:q0 + NI[c]],
                                 qk_hi["k", r][rows, b * TP:(b + 1) * TP], qk_lo["k", r][rows, b * TP:(b + 1) * TP])
                last.then_inc(z_done, 1)

            def pe_body(pe, body):
                for s in range(SLOTS):
                    if body.f and s < BLOCKS:
                        e, fb = divmod(s, FB)
                        cols = slice(e * WCH + fb * P, e * WCH + (fb + 1) * P)
                        if s == 0:
                            pe.wait_ge(x2_done, body.at(1, f=1))
                            if body.i is None and body.nf == 0:
                                pe.wait_ge(w_lo_done, NE)
                        wait(pe, gelu_done, body.at(s, f=BLOCKS))
                        three(up[:, 0:NT], ew_hi[:, cols], ew_lo[:, cols], x2_hi[:], x2_lo[:]).then_inc(up_done, 1)
                    if body.h and scores_at(s) is not None:
                        pe_scores(pe, body, scores_at(s), this_group(body))
                    if body.n and s == SCORES0_AT:
                        pe_scores(pe, body, 0, next_group(body))
                    if body.f and 0 <= s - LAG < BLOCKS:
                        d = s - LAG
                        e, fb = divmod(d, FB)
                        cols = slice(e * WCH + 512 + fb * P, e * WCH + 512 + (fb + 1) * P)
                        if (d % FB == 0 and e != 1):
                            wait(pe, comb_done, body.at(max(e - 1, 0), f=9))
                        pe.wait_ge(g_lo_done, body.at(d + 1, f=BLOCKS))
                        last = three(dn[:, 0:NT], ew_hi[:, cols], ew_lo[:, cols], g_hi[d % 4][:], g_lo[d % 4][:],
                                     start=fb == 0 and e != 1, stop=fb == FB - 1 and e > 1)
                        if e == 1 and fb == FB - 1:
                            wait_read(pe, body, use_of(body, "cwT", 0))
                            last = three(dn[:, 0:NT], rb2_hi[:], rb2_lo[:], cwT_hi[:], cwT_lo[:], start=False)
                        if fb == FB - 1 and e >= 1:
                            last.then_inc(dn_done, 1)
                    u = transposes_at(s)
                    if body.h and u is not None:
                        wait(pe, at_lo_done, body.at(u, h=UNITS))
                        pe.wait_ge(relu_done, body.at(u + 1, h=UNITS))
                        for jc in range(2):
                            for c in range(2):
                                last = nc.tensor.transpose(
                                    at[0:NI[jc], jc * TP + c * IC:jc * TP + c * IC + NI[c]],
                                    a[u % 2][0:NI[c], c, jc * IC:jc * IC + NI[jc]], ident[0:NI[c], 0:NI[c]])
                        last.then_inc(at_done, 1)
                    u = values_at(s)
                    if body.h and u is not None:
                        p, b, j = head_of(u)
                        cols = slice((2 * p + j) * P, (2 * p + j + 1) * P)
                        pe.wait_ge(at_lo_done, body.at(u + 1, h=UNITS))
                        if u == 0:
                            wait(pe, h2_done, body.at(0, h=1))
                        for jc in range(2):
                            n = NI[jc]
                            last = three(y[:, b * TP:(b + 1) * TP], v_hi[0:n, b, jc, cols], v_lo[0:n, b, jc, cols],
                                         at_hi[u % 2][0:n, jc, :], at_lo[u % 2][0:n, jc, :],
                                         start=u == 0 and jc == 0, stop=p == 3 and j == 1 and jc == 1, share=True)
                        if u == UNITS - 1:
                            last.then_inc(y_done, 1)
                    if body.h and s in LN2:
                        what = LN2[s]
                        if what == "var":
                            pe.wait_ge(ln2_sq, body.at(1, h=1))
                        else:
                            pe.wait_ge(ln2_rs, body.at(1, h=1))
                        ln_product(pe, z[1], what, h2).then_inc(ln2_pe, 1)
                    for k, _, what, arg in uses(body, s):
                        pe_shared(pe, body, k, what, arg)

            def act_shared(act, body, k, what, arg):
                sh = shb[sh_bank(body, k)]
                if what in HAS_HI:
                    act.wait_ge(sh_done, sh_at(body, k + 1))
                    if what == "v":
                        b, c, half = arg
                        dst, src = v_hi[:, b, c, half * HALF:(half + 1) * HALF], sh[0:IC, :]
                    elif what == "cwT":
                        dst, src = cwT_hi[:], sh[0:NEXP, 0:NT]
                    else:
                        dst, src = qk_hi[what, arg % 2][:], sh[:, 0:NT]
                    nc.scalar.activation(dst, src, ACT.Copy,
                                         scale=DH ** -0.5 if what == "q" else 1.0).then_inc(sh_hi, 1)
                elif what == "cwB":
                    wait(act, comb_done, body.at(arg, f=9))
                    act.wait_ge(sh_done, sh_at(body, k + 1))
                    nc.scalar.activation(cwB[arg % 2], sh[:, 0:NT], ACT.Copy).then_inc(sh_free[sh_bank(body, k)], 1)

            def act_attention(act, u, count):
                act.wait_ge(ntau_done, count(u + 1, UNITS))
                for c in range(2):
                    last = nc.scalar.activation(a[u % 2][0:NI[c], c, 0:T], z[u % 2][0:NI[c], c * TP:c * TP + T],
                                                ACT.Relu, bias=ntau[u % 2][0:NI[c], c:c + 1])
                last.then_inc(relu_done, 1)

            def act_body(act, body):
                for s in range(SLOTS):
                    if loads_weights(body) and s % 4 == 3 and s // 4 < NE:
                        act_weights(act, s // 4)
                    if body.f and s < BLOCKS:
                        wait(act, g_lo_done, body.at(s - 1, f=BLOCKS))
                        act.wait_ge(up_done, body.at(s + 1, f=BLOCKS))
                        nc.scalar.activation(g_raw[s % 2], up[:, 0:NT], ACT.Gelu,
                                             bias=up_bias[:, s:s + 1]).then_inc(gelu_done, 1)
                    if body.f and s == EXP_AT:
                        act.wait_ge(lg_done, body.at(1, f=1))
                        nc.scalar.activation(ex[:], lg[:], ACT.Exp).then_inc(ex_done, 1)
                    if body.h and attention_at(s):
                        act_attention(act, attention_at(s), this_group(body))
                    if body.n and s == ATTENTION0_AT:
                        act_attention(act, 0, next_group(body))
                    if body.f and s < BLOCKS and act_rounds(s):
                        act.wait_ge(gelu_done, body.at(s + 1, f=BLOCKS))
                        nc.scalar.activation(g_hi[s % 4][:], g_raw[s % 2], ACT.Copy).then_inc(g_hi_act, 1)
                    u = transposes_at(s)
                    if body.h and u is not None:
                        act.wait_ge(at_done, body.at(u + 1, h=UNITS))
                        nc.scalar.activation(at_hi[u % 2][:, :, 0:T], at[0:IC, 0:NT].rearrange("p (c t) -> p c t", c=2)[:, :, 0:T],
                                             ACT.Copy).then_inc(at_hi_done, 1)
                    if body.n and s == SQUARE1_AT:
                        act.wait_ge(ln1_xc, body.at(1, n=1))
                        nc.scalar.activation(sq[:], xc[:], ACT.Square).then_inc(ln1_sq, 1)
                    if body.h and s == SQUARE2_AT:
                        act.wait_ge(ln2_xc, body.at(1, h=1))
                        nc.scalar.activation(sq[:], xc[:], ACT.Square).then_inc(ln2_sq, 1)
                    for k, _, what, arg in uses(body, s):
                        act_shared(act, body, k, what, arg)

            def act_weights(act, e):
                act.wait_ge(w_loaded[e % 2], 16 * (e // 2 + 1))
                nc.scalar.activation(ew_hi[:, e * WCH:(e + 1) * WCH], wst[e % 2], ACT.Copy).then_inc(w_hi_done, 1)

            def pool_weights(pool, e):
                pool.wait_ge(w_hi_done, e + 1)
                nc.gpsimd.tensor_tensor(ew_lo[:, e * WCH:(e + 1) * WCH], wst[e % 2],
                                        ew_hi[:, e * WCH:(e + 1) * WCH].bitcast(F32),
                                        ALU.subtract).then_inc(w_lo_done, 1)

            def dve_shared(dve, body, k, khi, what, arg):
                sh, free = shb[sh_bank(body, k)], sh_free[sh_bank(body, k)]
                done = sh_at(body, k + 1)
                if what in HAS_HI:
                    dve.wait_ge(sh_hi, sh_hi_at(body, khi + 1))
                    if what == "v":
                        b, c, half = arg
                        cols = slice(half * HALF, (half + 1) * HALF)
                        nc.vector.tensor_tensor(v_lo[:, b, c, cols], sh[0:IC, :], v_hi[:, b, c, cols].bitcast(F32),
                                                ALU.subtract).then_inc(free, 1)
                    elif what == "q":
                        nc.vector.scalar_tensor_tensor(
                            out=qk_lo["q", arg % 2][:], in0=sh[:, 0:NT], scalar=DH ** -0.5,
                            in1=qk_hi["q", arg % 2][:].bitcast(F32), op0=ALU.mult, op1=ALU.subtract).then_inc(free, 1)
                    elif what == "k":
                        nc.vector.tensor_tensor(qk_lo["k", arg % 2][:], sh[:, 0:NT], qk_hi["k", arg % 2][:].bitcast(F32),
                                                ALU.subtract).then_inc(free, 1)
                    else:
                        nc.vector.tensor_tensor(cwT_lo[:], sh[0:NEXP, 0:NT], cwT_hi[:].bitcast(F32),
                                                ALU.subtract).then_inc(free, 1)
                elif what == "logits":
                    dve.wait_ge(sh_done, done)
                    nc.vector.tensor_tensor(lg[:], sh[0:IC, 0:4 * NEXP].rearrange("p (c e) -> p c e", c=4),
                                            gb[0:IC, :].unsqueeze(1).broadcast_to([IC, 4, NEXP]),
                                            ALU.add).then_inc(free, 1)
                    dve.drain()
                    nc.vector.tensor_reduce(lmax[:], lg[:], AX.X, ALU.max)
                    dve.drain()
                    nc.vector.tensor_tensor(lg[:], lg[:], lmax[:].unsqueeze(2).broadcast_to([IC, 4, NEXP]),
                                            ALU.subtract).then_inc(lg_done, 1)
                elif what == "mean":
                    dve.wait_ge(sh_done, done)
                    nc.vector.tensor_tensor(xc[:], h_next[:], sh[:, 0:NT], ALU.subtract).then_inc(ln1_xc, 1)
                    nc.vector.drain().then_inc(free, 1)
                elif what == "mean2":
                    dve.wait_ge(sh_done, done)
                    nc.vector.tensor_tensor(xc[:], h2[:], sh[:, 0:NT], ALU.subtract).then_inc(ln2_xc, 1)
                    nc.vector.drain().then_inc(free, 1)
                elif what == "var":
                    dve.wait_ge(sh_done, done)
                    nc.vector.tensor_scalar(ve[:], sh[0:IC, 0:4], EPS, None, ALU.add).then_inc(ln1_ve, 1)
                    nc.vector.drain().then_inc(free, 1)
                elif what == "spread":
                    dve.wait_ge(sh_done, done)
                    nc.vector.tensor_tensor(xc[:], xc[:], sh[:, 0:NT], ALU.mult)
                    dve.drain()
                    nc.vector.tensor_copy(x1_hi[:], xc[:])
                    dve.drain()
                    nc.vector.tensor_tensor(x1_lo[:], xc[:], x1_hi[:].bitcast(F32), ALU.subtract).then_inc(free, 1)

            def softmax(dve, body):
                dve.wait_ge(ex_done, body.at(1, f=1))
                nc.vector.tensor_reduce(lsum[:], ex[:], AX.X, ALU.add)
                dve.drain()
                nc.vector.reciprocal(lrec[:], lsum[:])
                dve.drain()
                nc.vector.tensor_tensor(pr[:], ex[:], lrec[:].unsqueeze(2).broadcast_to([IC, 4, NEXP]),
                                        ALU.mult)
                dve.drain()
                nc.vector.tensor_tensor(bigger[:].rearrange("p c (i e) -> p c i e", i=NEXP),
                                        pr[:].unsqueeze(3).broadcast_to([IC, 4, NEXP, NEXP]),
                                        pr[:].unsqueeze(2).broadcast_to([IC, 4, NEXP, NEXP]),
                                        ALU.is_gt).then_inc(bigger_done, 1)

            def top2(dve, body):
                dve.wait_ge(pairs_done, body.at(1, f=1))
                nc.vector.tensor_reduce(s_col[:], pairs[:].rearrange("p c (i e) -> p c e i", i=NEXP), AX.X, ALU.add)
                nc.vector.tensor_reduce(s_row[:], pairs[:].rearrange("p c (i e) -> p c i e", i=NEXP), AX.X, ALU.add)
                dve.drain()
                nc.vector.tensor_tensor(rank[:], s_col[:], s_row[:], ALU.subtract)
                dve.drain()
                nc.vector.tensor_tensor(rank[:], rank[:], e_index[:].rearrange("p (c e) -> p c e", c=4), ALU.add)
                dve.drain()
                nc.vector.scalar_tensor_tensor(out=cw[:], in0=rank[:], scalar=1.5, in1=pr[:],
                                               op0=ALU.is_lt, op1=ALU.mult).then_inc(cw_done, 1)

            def threshold(dve, u, newton, count):
                zu, cd = z[u % 2], cand[u % 2]
                def own(n):
                    dve.wait_ge(z_read, count(3 * u + n, 3 * UNITS))
                wait(dve, over_done, count(u - 1, UNITS))
                dve.wait_ge(z_done, count(u + 1, UNITS))
                dve.nop(nofuse=True)
                for c in range(2):
                    nc.vector.max(cd[0:NI[c], c, 0:8], zu[0:NI[c], c * TP:c * TP + T])
                dve.drain()
                for c in range(2):
                    nc.vector.match_replace(z_rest[c][0:NI[c], :], cd[0:NI[c], c, 0:8],
                                            zu[0:NI[c], c * TP:c * TP + T], NEG)
                dve.drain()
                for c in range(2):
                    last = nc.vector.max(cd[0:NI[c], c, 8:16], z_rest[c][0:NI[c], :])
                last.then_inc(z_read, 1)
                own(1)
                nc.vector.tensor_tensor_scan(sums[:], seg[:], cd[:].rearrange("p c r -> p (c r)"), 0.0,
                                             ALU.mult, ALU.add).then_inc(z_read, 1)
                own(2)
                nc.vector.scalar_tensor_tensor(out=taus[:], in0=sums[:], scalar=-1.0, in1=rinv[:],
                                               op0=ALU.add, op1=ALU.mult).then_inc(z_read, 1)
                own(3)
                i = nc.vector.tensor_reduce(ntau[u % 2][:], taus[:].rearrange("p (c r) -> p c r", c=2), AX.X, ALU.max,
                                            negate=True)
                if newton:
                    dve.drain()
                    with dve.Fori(0, NEWTON) as _:
                        for c in range(2):
                            n = NI[c]
                            zc, nt = zu[0:n, c * TP:c * TP + T], ntau[u % 2][0:n, c:c + 1]
                            nc.vector.tensor_scalar(z_rest[c][0:n, :], zc, nt, 0.0, ALU.add, ALU.max)
                            dve.drain()
                            nc.vector.tensor_reduce(nsum[0:n, c:c + 1], z_rest[c][0:n, :], AX.X, ALU.add)
                            dve.drain()
                            nc.vector.tensor_scalar(z_rest[c][0:n, :], z_rest[c][0:n, :], 0.0, None, ALU.is_gt)
                            dve.drain()
                            nc.vector.tensor_reduce(ncnt[0:n, c:c + 1], z_rest[c][0:n, :], AX.X, ALU.add)
                            dve.drain()
                            nc.vector.reciprocal(nrec[0:n, c:c + 1], ncnt[0:n, c:c + 1])
                            dve.drain()
                            nc.vector.scalar_tensor_tensor(out=nsum[0:n, c:c + 1], in0=nsum[0:n, c:c + 1], scalar=-1.0,
                                                           in1=nrec[0:n, c:c + 1], op0=ALU.add, op1=ALU.mult)
                            dve.drain()
                            nc.vector.tensor_tensor(nt, nt, nsum[0:n, c:c + 1], ALU.subtract)
                            dve.drain()
                    i = nc.vector.tensor_copy(nrec[0:1, 0:1], nrec[0:1, 0:1])
                i.then_inc(ntau_done, 1)

            def dve_body(dve, body, newton):
                for s in range(SLOTS + 1):
                    if body.f and s < BLOCKS and not act_rounds(s):
                        dve.wait_ge(gelu_done, body.at(s + 1, f=BLOCKS))
                        nc.vector.tensor_copy(g_hi[s % 4][:], g_raw[s % 2]).then_inc(g_hi_dve, 1)
                    if body.f and s >= 10 and (s - 10) % 4 == 0 and (s - 10) // 4 <= NEXP:
                        c = (s - 10) // 4
                        if c == 0:
                            wait(dve, out_stored, body.at(0, f=1) * 16)
                            dve.wait_ge(dn_done, body.at(1, f=9))
                            nc.vector.scalar_tensor_tensor(out=acc[:], in0=dn[:, 0:NT], scalar=sb2_sum[:], in1=h2[:],
                                                           op0=ALU.add, op1=ALU.add).then_inc(comb_done, 1)
                        else:
                            e = c - 1
                            wait_read(dve, body, use_of(body, "cwB", e))
                            wait(dve, acc_done, body.at(e - 1, f=8))
                            dve.wait_ge(dn_done, body.at(c + 1, f=9))
                            nc.vector.tensor_tensor(tmp[e % 2], dn[:, 0:NT], cwB[e % 2], ALU.mult).then_inc(comb_done, 1)
                    u = transposes_at(s)
                    if body.h and u is not None:
                        dve.wait_ge(at_hi_done, body.at(u + 1, h=UNITS))
                        nc.vector.tensor_tensor(at_lo[u % 2][:, :, 0:T], at[0:IC, 0:NT].rearrange("p (c t) -> p c t", c=2)[:, :, 0:T],
                                                at_hi[u % 2][:, :, 0:T].bitcast(F32), ALU.subtract).then_inc(at_lo_done, 1)
                    if body.h and scores_at(s) is not None:
                        threshold(dve, scores_at(s), newton, this_group(body))
                    if body.h and s == OUT_AT:
                        dve.wait_ge(res_loaded, body.at(1, h=1) * 16)
                        dve.wait_ge(y_done, body.at(1, h=1))
                        nc.vector.scalar_tensor_tensor(out=h2[:], in0=y[:, 0:NT], scalar=bo[:], in1=h_res[:],
                                                       op0=ALU.add, op1=ALU.add).then_inc(h2_done, 1)
                    if body.h and s in LN2:
                        dve.wait_ge(ln2_pe, body.at({"var": 1, "spread": 2}[LN2[s]], h=2))
                        if LN2[s] == "var":
                            nc.vector.tensor_scalar(ve[:], z[1][0:IC, 0:4], EPS, None, ALU.add).then_inc(ln2_ve, 1)
                        else:
                            nc.vector.tensor_tensor(xc[:], xc[:], z[1][:, 0:NT], ALU.mult)
                            dve.drain()
                            nc.vector.tensor_copy(x2_hi[:], xc[:])
                            dve.drain()
                            nc.vector.tensor_tensor(x2_lo[:], xc[:], x2_hi[:].bitcast(F32), ALU.subtract).then_inc(x2_done, 1)
                    if body.f and s == SOFTMAX_AT:
                        softmax(dve, body)
                    if body.f and s == TOP2_AT:
                        top2(dve, body)
                    if body.n and s == SCORES0_AT:
                        threshold(dve, 0, newton, next_group(body))
                    for k, khi, what, arg in uses(body, s):
                        dve_shared(dve, body, k, khi, what, arg)

            def pool_body(pool, body):
                for s in range(SLOTS + 1):
                    if loads_weights(body) and s % 4 == 3 and s // 4 < NE:
                        pool_weights(pool, s // 4)
                    for _, _, what, _ in uses(body, s):
                        if what == "var":
                            pool.wait_ge(ln1_ve, body.at(1, n=1))
                            nc.gpsimd.tensor_tensor(rs[:], ve[:], mhalf[:], ALU.pow).then_inc(ln1_rs, 1)
                    if body.h and LN2.get(s) == "var":
                        pool.wait_ge(ln2_ve, body.at(1, h=1))
                        nc.gpsimd.tensor_tensor(rs[:], ve[:], mhalf[:], ALU.pow).then_inc(ln2_rs, 1)
                    if body.f and s < BLOCKS:
                        pool.wait_ge(*g_hi_ready(body, s))
                        nc.gpsimd.tensor_tensor(g_lo[s % 4][:], g_raw[s % 2], g_hi[s % 4][:].bitcast(F32),
                                                ALU.subtract).then_inc(g_lo_done, 1)
                    if body.f and s == SOFTMAX_AT:
                        pool.wait_ge(bigger_done, body.at(1, f=1))
                        nc.gpsimd.tensor_tensor(pairs[:], bigger[:], later[:].unsqueeze(1).broadcast_to([IC, 4, NEXP * NEXP]),
                                                ALU.mult).then_inc(pairs_done, 1)
                    u = attention_at(s)
                    if body.h and u is not None:
                        pool.wait_ge(ntau_done, body.at(u + 1, h=UNITS))
                        nc.gpsimd.tensor_tensor(over[:], cand[u % 2][:, :, 15], ntau[u % 2][:], ALU.add).then_inc(over_done, 1)
                        pool.drain()
                        nc.gpsimd.tensor_scalar(over[:], over[:], 0.0, None, ALU.is_gt)
                        pool.drain()
                        nc.gpsimd.tensor_tensor(worst[:], worst[:], over[:], ALU.add)
                        pool.drain()
                    if body.f and s >= 15 and (s - 15) % 4 == 0 and (s - 15) // 4 < NEXP:
                        e = (s - 15) // 4
                        if e == NEXP - 1:
                            pool.drain()
                        pool.wait_ge(comb_done, body.at(e + 2, f=9))
                        nc.gpsimd.tensor_tensor(acc[:], acc[:], tmp[e % 2], ALU.add).then_inc(acc_done, 1)

            with nc.Block() as block:
                @block.sync
                def _(sp):
                    bodies(sp, lambda b, nw: sp_body(sp, b), 0, False)
                    sp.wait_ge(out_stored, 16 * G)
                    sp.wait_ge(flag_done, 1)
                    rows = sp.value_load(flag[0:1, 0:1])
                    either(sp, rows, lambda: (bodies(sp, lambda b, nw: sp_body(sp, b), 1, True),
                                              sp.wait_ge(out_stored, 32 * G)))

                @block.scalar
                def _(act):
                    act.wait_ge(ready, 1)
                    bodies(act, lambda b, nw: act_body(act, b), 0, False)
                    act.wait_ge(flag_done, 1)
                    rows = act.value_load(flag[0:1, 0:1])
                    either(act, rows, lambda: bodies(act, lambda b, nw: act_body(act, b), 1, True))

                @block.gpsimd
                def _(pool):
                    pool.wait_ge(ready, 1)
                    bodies(pool, lambda b, nw: pool_body(pool, b), 0, False)
                    pool.drain().then_inc(worst_done, 1)
                    pool.wait_ge(flag_done, 1)
                    rows = pool.value_load(flag[0:1, 0:1])
                    either(pool, rows, lambda: bodies(pool, lambda b, nw: pool_body(pool, b), 1, True))

                @block.vector
                def _(dve):
                    nc.vector.memset(at[:], 0.0)
                    for r in range(2):
                        nc.vector.memset(at_hi[r][:, :, T:TP].bitcast(F32), 0.0)
                        nc.vector.memset(at_lo[r][:, :, T:TP].bitcast(F32), 0.0)
                        nc.vector.memset(cand[r][:], 0.0)
                    dve.drain()
                    nc.vector.memset(nrec[:], 1.0).then_inc(ready, 1)
                    bodies(dve, lambda b, nw: dve_body(dve, b, nw), 0, False)
                    dve.wait_ge(worst_done, 1)
                    nc.vector.tensor_scalar(nsum[:], worst[:], 0.0, float(P), ALU.is_gt, ALU.mult)
                    nc.vector.drain().then_inc(flag_sum, 1)
                    dve.wait_ge(flag_sum, 2)
                    nc.vector.tensor_copy(flag[:], shb[0][0:1, 0:1]).then_inc(flag_done, 1)
                    dve.wait_ge(flag_done, 1)
                    rows = dve.value_load(flag[0:1, 0:1])
                    either(dve, rows, lambda: bodies(dve, lambda b, nw: dve_body(dve, b, nw), 1, True))

                @block.tensor
                def _(pe):
                    pe.wait_ge(ready, 1)
                    bodies(pe, lambda b, nw: pe_body(pe, b), 0, False)
                    pe.wait_ge(flag_sum, 1)
                    for c in range(2):
                        last = nc.tensor.matmul(shb[0][0:1, 0:1], nsum[0:NI[c], c:c + 1], mean_w[0:NI[c], 0:1],
                                                start=c == 0, stop=c == 1)
                    last.then_inc(flag_sum, 1)
                    pe.wait_ge(flag_done, 1)
                    rows = pe.value_load(flag[0:1, 0:1])
                    either(pe, rows, lambda: bodies(pe, lambda b, nw: pe_body(pe, b), 1, True))


def kernel(x, L0_tok_W0, L0_tok_b0, L0_tok_pos0, L0_tok_W1, L0_tok_b1, L0_tok_pos1, L0_tok_W2, L0_tok_b2,
           L0_tok_pos2, L0_tok_scale_emb, L0_attn_W_qkv, L0_attn_W_out, L0_attn_b_out, L0_ffn_gate_w,
           L0_ffn_gate_b, L0_ffn_sw1, L0_ffn_sb1, L0_ffn_sw2, L0_ffn_sb2, L0_ffn_rw1, L0_ffn_rb1,
           L0_ffn_rw2, L0_ffn_rb2):
    import numpy as np
    import concourse.bacc as bacc
    from concourse.bass_utils import run_bass_kernel_spmd

    def arr(v):
        return np.asarray(v)

    xt = arr(x).reshape(G, NB, CTX // 4, 4, P).transpose(0, 4, 1, 3, 2)
    xT = np.zeros((G, P, NB, XR, XM), xt.dtype)
    xT[..., :CTX // 4] = xt

    def patch_weights(w, p):
        return arr(w).reshape(P, p, P).transpose(2, 1, 0).reshape(P, p * P)

    def column(v):
        return arr(v).reshape(-1, 1)

    wqkv = arr(L0_attn_W_qkv)
    inner = HEADS * DH
    w1 = np.concatenate([arr(L0_ffn_sw1), arr(L0_ffn_rw1)])
    w2 = np.concatenate([arr(L0_ffn_sw2), arr(L0_ffn_rw2)])
    up_w = w1.transpose(0, 2, 1)
    dn_w = w2.reshape(-1, P, FB, P).transpose(0, 3, 2, 1).reshape(-1, P, FF)
    ins = {
        "xT": xT.reshape(G, P, NB * XB),
        "w0T": patch_weights(L0_tok_W0, PATCH[0]),
        "w1T": patch_weights(L0_tok_W1, PATCH[1]),
        "w2T": patch_weights(L0_tok_W2, PATCH[2]),
        "posT": np.concatenate([arr(v)[0] for v in (L0_tok_pos0, L0_tok_pos1, L0_tok_pos2)]).T,
        "b0": column(L0_tok_b0), "b1": column(L0_tok_b1), "b2": column(L0_tok_b2),
        "seT": arr(L0_tok_scale_emb).T,
        "wqkT": wqkv[:, :2 * inner],
        "wvT": wqkv[:, 2 * inner:].reshape(P, HEADS, DH).transpose(2, 1, 0).reshape(DH, HEADS * P),
        "woutT": arr(L0_attn_W_out).reshape(HEADS, DH, P).transpose(1, 0, 2).reshape(DH, HEADS * P),
        "b_out": column(L0_attn_b_out),
        "gateT": arr(L0_ffn_gate_w).T,
        "gate_b": arr(L0_ffn_gate_b),
        "ew": np.concatenate([up_w, dn_w], axis=2),
        "eb1": np.concatenate([arr(L0_ffn_sb1), arr(L0_ffn_rb1)]).reshape(BLOCKS, P).T,
        "sb2T": arr(L0_ffn_sb2).T,
        "rb2": arr(L0_ffn_rb2),
    }
    nc = bacc.Bacc("TRN2", target_bir_lowering=False, num_devices=1)
    arrays, args = {}, []
    for name, v in ins.items():
        v = np.ascontiguousarray(v)
        arrays[f"in_{name}"] = v
        args.append(nc.dram_tensor(f"in_{name}", v.shape, mybir.dt.from_np(v.dtype), kind="ExternalInput").ap())
    out = nc.dram_tensor("out_T", (G, P, NT), F32, kind="ExternalOutput").ap()
    build(nc, *args, out)
    r = run_bass_kernel_spmd(nc, [arrays], core_ids=[0])
    got = r.results[0]["out_T"].reshape(G, P, NB, TP)[..., :T]
    return np.ascontiguousarray(got.transpose(0, 2, 3, 1).reshape(BATCH, T, P))
```
